# Optimizing a Trainium2 kernel written in Bass

```python
import numpy as np
import jax
import jax.numpy as jnp

def _softmax(x, axis=-1):
    return jax.nn.softmax(x, axis=axis)

def _gelu(x):
    return jax.nn.gelu(x, approximate=True)

def _silu(x):
    return jax.nn.silu(x)

def _sigmoid(x):
    return jax.nn.sigmoid(x)

def _layernorm(x, axis=-1, eps=1e-05):
    m = jnp.mean(x, axis=axis, keepdims=True)
    v = jnp.var(x, axis=axis, keepdims=True)
    return (x - m) / jnp.sqrt(v + eps)

def _scatter_add(tgt, idx, src, axis=0):
    return tgt.at[idx].add(src)

def _segment_sum(src, seg, n):
    return jax.ops.segment_sum(src, seg, n)
kernel_name = 'mk_adaln_d1_jaxref_r8_9651f8'

def setup_inputs(seed: int=0):
    np.random.seed(seed)
    _w = jnp.asarray

    def _L0_attn_setup():
        import jax, jax.numpy as jnp
        import numpy as np
        D_MODEL = 128
        N_HEADS = 16
        HEAD_DIM = D_MODEL // N_HEADS
        EPS_ATTN = 1e-06
        EPS_LN = 1e-05

        def layer_norm(x, gamma, beta):
            mu = jnp.mean(x, axis=-1, keepdims=True)
            var = jnp.var(x, axis=-1, keepdims=True)
            return (x - mu) * jax.lax.rsqrt(var + EPS_LN) * gamma + beta

        def linear_attention(x, Wq, bq, Wk, bk, Wv, bv, Wo, bo):
            N, L, _ = x.shape
            H, Dh = (N_HEADS, HEAD_DIM)
            Q = (x @ Wq + bq).reshape(N, L, H, Dh)
            K = (x @ Wk + bk).reshape(N, L, H, Dh)
            V = (x @ Wv + bv).reshape(N, L, H, Dh)
            Q = jax.nn.elu(Q) + 1.0
            K = jax.nn.elu(K) + 1.0
            KV = jnp.einsum('nshd,nshm->nhmd', K, V)
            Ksum = K.sum(axis=1)
            Z = 1.0 / (jnp.einsum('nlhd,nhd->nlh', Q, Ksum) + EPS_ATTN)
            out = jnp.einsum('nlhd,nhmd,nlh->nlhm', Q, KV, Z)
            out = out.reshape(N, L, H * Dh)
            return out @ Wo + bo
        key = jax.random.key(seed)
        ks = jax.random.split(key, 16)
        s = 1.0 / np.sqrt(D_MODEL)
        inp = {'x': jax.random.normal(ks[0], (4, 512, D_MODEL), dtype=jnp.float32), 'Wq': jax.random.normal(ks[1], (D_MODEL, D_MODEL), dtype=jnp.float32) * s, 'bq': jnp.zeros((D_MODEL,), jnp.float32), 'Wk': jax.random.normal(ks[2], (D_MODEL, D_MODEL), dtype=jnp.float32) * s, 'bk': jnp.zeros((D_MODEL,), jnp.float32), 'Wv': jax.random.normal(ks[3], (D_MODEL, D_MODEL), dtype=jnp.float32) * s, 'bv': jnp.zeros((D_MODEL,), jnp.float32), 'Wo': jax.random.normal(ks[4], (D_MODEL, D_MODEL), dtype=jnp.float32) * s, 'bo': jnp.zeros((D_MODEL,), jnp.float32), 'W1': jax.random.normal(ks[5], (D_MODEL, 4 * D_MODEL), dtype=jnp.float32) * s, 'b1': jnp.zeros((4 * D_MODEL,), jnp.float32), 'W2': jax.random.normal(ks[6], (4 * D_MODEL, D_MODEL), dtype=jnp.float32) * (0.5 * s), 'b2': jnp.zeros((D_MODEL,), jnp.float32), 'g1': jnp.ones((D_MODEL,), jnp.float32), 'beta1': jnp.zeros((D_MODEL,), jnp.float32), 'g2': jnp.ones((D_MODEL,), jnp.float32), 'beta2': jnp.zeros((D_MODEL,), jnp.float32)}
        return inp
    _L0_attn_in = _L0_attn_setup()

    def _L0_ffn_setup():
        import jax, jax.numpy as jnp
        import numpy as np
        DIM = 128

        def _reference_tuple_inner(x, W_r, W_k, W_v, mu_r, mu_k):
            B, T, C = x.shape
            x_prev = jnp.concatenate([jnp.zeros((B, 1, C), x.dtype), x[:, :-1, :]], axis=1)
            xr = mu_r * x + (1.0 - mu_r) * x_prev
            xk = mu_k * x + (1.0 - mu_k) * x_prev
            r = jax.nn.sigmoid(jnp.einsum('btc,dc->btd', xr, W_r))
            k = jnp.einsum('btc,dc->btd', xk, W_k)
            k_act = jnp.square(jax.nn.relu(k))
            out = r * jnp.einsum('btc,dc->btd', k_act, W_v)
            new_state = x[:, -1, :]
            return (out, new_state)
        key = jax.random.key(seed)
        ks = jax.random.split(key, 6)
        B, T, C = (8, 256, DIM)
        x = jax.random.normal(ks[0], (B, T, C), dtype=jnp.float32)
        s = 1.0 / np.sqrt(C)
        W_r = jax.random.uniform(ks[1], (C, C), jnp.float32, -s, s)
        W_k = jax.random.uniform(ks[2], (C, C), jnp.float32, -s, s)
        W_v = jax.random.uniform(ks[3], (C, C), jnp.float32, -s, s)
        mu_r = jax.random.uniform(ks[4], (C,), jnp.float32)
        mu_k = jax.random.uniform(ks[5], (C,), jnp.float32)
        return {'x': x, 'W_r': W_r, 'W_k': W_k, 'W_v': W_v, 'mu_r': mu_r, 'mu_k': mu_k}
    _L0_ffn_in = _L0_ffn_setup()
    _L0_c = _w((lambda *s: np.random.randn(*s).astype(np.float32) * 0.05)(16, 128))
    _L0_wmod = _w((lambda *s: np.random.randn(*s).astype(np.float32) * 0.05)(128, 6 * 128) * 128 ** (-0.5))
    _d = {'L0_attn_x': _L0_attn_in['x'], 'L0_attn_Wq': _L0_attn_in['Wq'], 'L0_attn_bq': _L0_attn_in['bq'], 'L0_attn_Wk': _L0_attn_in['Wk'], 'L0_attn_bk': _L0_attn_in['bk'], 'L0_attn_Wv': _L0_attn_in['Wv'], 'L0_attn_bv': _L0_attn_in['bv'], 'L0_attn_Wo': _L0_attn_in['Wo'], 'L0_attn_bo': _L0_attn_in['bo'], 'L0_attn_W1': _L0_attn_in['W1'], 'L0_attn_b1': _L0_attn_in['b1'], 'L0_attn_W2': _L0_attn_in['W2'], 'L0_attn_b2': _L0_attn_in['b2'], 'L0_attn_g1': _L0_attn_in['g1'], 'L0_attn_beta1': _L0_attn_in['beta1'], 'L0_attn_g2': _L0_attn_in['g2'], 'L0_attn_beta2': _L0_attn_in['beta2'], 'L0_ffn_W_r': _L0_ffn_in['W_r'], 'L0_ffn_W_k': _L0_ffn_in['W_k'], 'L0_ffn_W_v': _L0_ffn_in['W_v'], 'L0_ffn_mu_r': _L0_ffn_in['mu_r'], 'L0_ffn_mu_k': _L0_ffn_in['mu_k'], 'L0_c': _L0_c, 'L0_wmod': _L0_wmod}
    _x0 = _d['L0_attn_x']
    _d['L0_attn_x'] = jax.random.normal(jax.random.fold_in(jax.random.key(seed), 1), (16, 256, 128), dtype=_x0.dtype)
    del _x0
    return _d

def reference(L0_attn_x, L0_attn_Wq, L0_attn_bq, L0_attn_Wk, L0_attn_bk, L0_attn_Wv, L0_attn_bv, L0_attn_Wo, L0_attn_bo, L0_attn_W1, L0_attn_b1, L0_attn_W2, L0_attn_b2, L0_attn_g1, L0_attn_beta1, L0_attn_g2, L0_attn_beta2, L0_ffn_W_r, L0_ffn_W_k, L0_ffn_W_v, L0_ffn_mu_r, L0_ffn_mu_k, L0_c, L0_wmod):

    def _L0_attn_ref(x, Wq, bq, Wk, bk, Wv, bv, Wo, bo, W1, b1, W2, b2, g1, beta1, g2, beta2):
        import jax, jax.numpy as jnp
        import numpy as np
        D_MODEL = 128
        N_HEADS = 16
        HEAD_DIM = D_MODEL // N_HEADS
        EPS_ATTN = 1e-06
        EPS_LN = 1e-05

        def layer_norm(x, gamma, beta):
            mu = jnp.mean(x, axis=-1, keepdims=True)
            var = jnp.var(x, axis=-1, keepdims=True)
            return (x - mu) * jax.lax.rsqrt(var + EPS_LN) * gamma + beta

        def linear_attention(x, Wq, bq, Wk, bk, Wv, bv, Wo, bo):
            N, L, _ = x.shape
            H, Dh = (N_HEADS, HEAD_DIM)
            Q = (x @ Wq + bq).reshape(N, L, H, Dh)
            K = (x @ Wk + bk).reshape(N, L, H, Dh)
            V = (x @ Wv + bv).reshape(N, L, H, Dh)
            Q = jax.nn.elu(Q) + 1.0
            K = jax.nn.elu(K) + 1.0
            KV = jnp.einsum('nshd,nshm->nhmd', K, V)
            Ksum = K.sum(axis=1)
            Z = 1.0 / (jnp.einsum('nlhd,nhd->nlh', Q, Ksum) + EPS_ATTN)
            out = jnp.einsum('nlhd,nhmd,nlh->nlhm', Q, KV, Z)
            out = out.reshape(N, L, H * Dh)
            return out @ Wo + bo
        x = x + linear_attention(x, Wq, bq, Wk, bk, Wv, bv, Wo, bo)
        x = layer_norm(x, g1, beta1)
        y = jax.nn.relu(x @ W1 + b1) @ W2 + b2
        return layer_norm(x + y, g2, beta2)

    def _L0_ffn_ref(x, W_r, W_k, W_v, mu_r, mu_k):
        import jax, jax.numpy as jnp
        import numpy as np
        DIM = 128

        def _reference_tuple_inner(x, W_r, W_k, W_v, mu_r, mu_k):
            B, T, C = x.shape
            x_prev = jnp.concatenate([jnp.zeros((B, 1, C), x.dtype), x[:, :-1, :]], axis=1)
            xr = mu_r * x + (1.0 - mu_r) * x_prev
            xk = mu_k * x + (1.0 - mu_k) * x_prev
            r = jax.nn.sigmoid(jnp.einsum('btc,dc->btd', xr, W_r))
            k = jnp.einsum('btc,dc->btd', xk, W_k)
            k_act = jnp.square(jax.nn.relu(k))
            out = r * jnp.einsum('btc,dc->btd', k_act, W_v)
            new_state = x[:, -1, :]
            return (out, new_state)
        return _reference_tuple_inner(x, W_r, W_k, W_v, mu_r, mu_k)[0]
    x = L0_attn_x
    mod = (_silu(L0_c) @ L0_wmod).reshape(L0_c.shape[0], 6, 1, -1)
    sa, ca, ga, sb, cb, gb = (mod[:, 0], mod[:, 1], mod[:, 2], mod[:, 3], mod[:, 4], mod[:, 5])
    ga = (2 * (ga >= 0) - 1) * jnp.maximum(jnp.abs(ga), 0.25)
    gb = (2 * (gb >= 0) - 1) * jnp.maximum(jnp.abs(gb), 0.25)
    h = _layernorm(x, axis=-1) * (1 + ca) + sa
    x = x + ga * _L0_attn_ref(h, L0_attn_Wq, L0_attn_bq, L0_attn_Wk, L0_attn_bk, L0_attn_Wv, L0_attn_bv, L0_attn_Wo, L0_attn_bo, L0_attn_W1, L0_attn_b1, L0_attn_W2, L0_attn_b2, L0_attn_g1, L0_attn_beta1, L0_attn_g2, L0_attn_beta2)
    h = _layernorm(x, axis=-1) * (1 + cb) + sb
    x = x + gb * _L0_ffn_ref(h, L0_ffn_W_r, L0_ffn_W_k, L0_ffn_W_v, L0_ffn_mu_r, L0_ffn_mu_k)
    return x

_drawn_inputs = setup_inputs


def setup_inputs(seed=0):
    import zlib

    import numpy as np

    out = dict(_drawn_inputs(seed))
    spreads = {'L0_attn_bq': (0.0, 0.8),
     'L0_attn_bk': (0.0, 0.8),
     'L0_attn_bv': (0.0, 0.352),
     'L0_attn_bo': (0.0, 0.343),
     'L0_attn_b1': (0.0, 0.601),
     'L0_attn_b2': (0.0, 0.404),
     'L0_attn_g1': (1.0, 0.2),
     'L0_attn_beta1': (0.0, 0.385),
     'L0_attn_g2': (1.0, 0.2),
     'L0_attn_beta2': (0.0, 0.312)}
    factors = {'L0_attn_Wq': 8.0,
     'L0_attn_Wk': 7.658,
     'L0_attn_Wv': 3.552,
     'L0_ffn_W_r': 8.0,
     'L0_ffn_W_k': 3.05,
     'L0_ffn_W_v': 2.807,
     'L0_ffn_mu_r': 8.0,
     'L0_ffn_mu_k': 4.788}
    for name, (base, spread) in spreads.items():
        noise = np.random.default_rng([zlib.crc32(name.encode()), seed]).standard_normal(out[name].shape)
        drawn = base * np.exp(spread * noise) if base else spread * noise
        out[name] = jnp.asarray(drawn.astype(out[name].dtype))
    for name, factor in factors.items():
        out[name] = (out[name] * factor).astype(out[name].dtype)
    return out
```

```python
from contextlib import ExitStack

import numpy as np

import concourse.bass as bass
from concourse import mybir

F32 = mybir.dt.float32
BF16 = mybir.dt.bfloat16
ALU = mybir.AluOpType
ACT = mybir.ActivationFunctionType

S, L, D = 16, 256, 128
NC = L // 128
H, DH = 16, 8
FF = 4
EPS_ATTN = 1e-6
EPS_LN = 1e-5
STEPS_DEEP = 4
CA, CB, SA, SB = range(4)
BV_ROW, G_ROW, GB_ROW, GATE_ROW = range(4)
ROWS = ("bq", "g1", "beta1", "b1", "mu_r", "mu_k")


def build(nc, a, out, scratch):
    with ExitStack() as ctx:
        def sb(name, shape, dt=F32):
            return ctx.enter_context(nc.sbuf_tensor(name, shape, dt))

        def sem(name):
            return ctx.enter_context(nc.semaphore(name))

        banks = [ctx.enter_context(nc.psum_tensor(f"bank{i}", [128, 512], F32)) for i in range(8)]

        wq, wk, wv, wo = (sb(n, [128, D]) for n in ("wq", "wk", "wv", "wo"))
        w1 = sb("w1", [128, FF * 128])
        w2 = sb("w2", [128, FF, D])
        wmod = sb("wmod", [128, 6 * D])
        mix_w = sb("mix_w", [128, 3, D])
        mix_wT = sb("mix_wT", [128, 3 * D])
        ident = sb("ident", [128, 128])
        ones = sb("ones", [128, 1])
        headmask = sb("headmask", [128, H, DH])
        power = sb("power", [128, NC])
        eps = sb("eps", [128, NC])
        ones3 = sb("ones3", [3, L], BF16)
        neg1 = sb("neg1", [128, 1])
        c_in = sb("c_in", [S, D])
        tanh_c = sb("tanh_c", [128, S])
        silu2 = sb("silu2", [128, S])
        siluT = sb("siluT", [128, S])
        modT = sb("modT", [128, 4 * S])
        vec_rows = sb("vec_rows", [8, 128])
        vec_cols = sb("vec_cols", [128, 8])
        row_in = sb("row_in", [S, 3, D])
        gate_sign = sb("gate_sign", [S, 2, D])
        gate_pos = sb("gate_pos", [S, 2, D])
        gate_size = sb("gate_size", [S, 2, D])
        gates = sb("gates", [S, 2, D])
        mod_rows = sb("mod_rows", [S, 4, D])
        bias3 = sb("bias3", [3, 4, D])
        part_hi = sb("part_hi", [3, 4, D], BF16)
        part_mid = sb("part_mid", [3, 4, D], BF16)
        part_lo = sb("part_lo", [3, 4, D], BF16)
        rest1 = sb("rest1", [3, 4, D])
        rest2 = sb("rest2", [3, 4, D])
        pick1 = sb("pick1", [3, 4, D])
        pick2 = sb("pick2", [3, 4, D])
        bias_parts = sb("bias_parts", [3, 4, D], BF16)
        x_all = sb("x_all", [128, S * NC, D])
        bv_row = [sb(f"bv_row{p}", [128, D]) for p in range(2)]
        gm_rows = [sb(f"gm_rows{p}", [128, 3, D]) for p in range(2)]
        n1 = [sb(f"n1_{p}", [128, NC, D]) for p in range(2)]
        hT = [sb(f"hT{p}", [128, L]) for p in range(2)]
        exp_k = sb("exp_k", [128, NC, D])
        k_sb = sb("k_sb", [128, NC, D])
        exp_q = sb("exp_q", [128, L])
        qT = sb("qT", [128, L])
        a_sb = sb("a_sb", [128, D + 1])
        wv_mod = sb("wv_mod", [128, D])
        ksum = a_sb[:, D:D + 1]
        kv_raw = sb("kv_raw", [128, D])
        kvs = sb("kvs", [128, D + H])
        den = sb("den", [128, NC, H])
        rden = sb("rden", [128, NC, H])
        att = sb("att", [128, NC, D])
        attT = sb("attT", [128, L])
        ny = sb("ny", [128, NC, D])
        x1T = sb("x1T", [128, L])
        hid = sb("hid", [128, FF, L])
        z1 = sb("z1", [128, NC, D])
        xb = sb("xb", [128, NC, D])
        x2 = [sb(f"x2_{p}", [128, NC, D]) for p in range(2)]
        n3 = sb("n3", [128, NC, D])
        h2T = sb("h2T", [128, 1 + L])
        diff = sb("diff", [128, L])
        xrT = sb("xrT", [128, L])
        xkT = sb("xkT", [128, L])
        tanh_r = sb("tanh_r", [128, NC, D])
        relu_k = sb("relu_k", [128, L])
        ksqT = sb("ksqT", [128, L])
        wv_gate = sb("wv_gate", [128, D])
        prod = sb("prod", [128, NC, D])
        out_sb = sb("out_sb", [128, NC, D])
        NORMS = ("n1", "ny", "z", "n3")
        stats = {n: sb(f"stats_{n}", [128, NC, 6]) for n in NORMS}
        mv = {n: sb(f"mv_{n}", [128, NC, 2]) for n in NORMS}
        vare = {n: sb(f"vare_{n}", [128, NC]) for n in NORMS}
        rstd = {n: sb(f"rstd_{n}", [128, NC]) for n in NORMS}

        x_in = [sem(f"x_in{i}") for i in range(4)]
        c_loaded, wmod_loaded, vec_loaded, kq_loaded = map(sem, ("c_loaded", "wmod_loaded", "vec_loaded", "kq_loaded"))
        wvo_loaded, w1_loaded, w2_loaded, mix_loaded = map(sem, ("wvo_loaded", "w1_loaded", "w2_loaded", "mix_loaded"))
        row_loaded, bias_loaded, rows_stored = map(sem, ("row_loaded", "bias_loaded", "rows_stored"))
        bv_in = [sem(f"bv_in{p}") for p in range(2)]
        gm_in = [sem(f"gm_in{p}") for p in range(2)]
        stored = sem("stored")
        const_pool, const_dve = sem("const_pool"), sem("const_dve")
        pe_setup, act_setup, dve_setup = sem("pe_setup"), sem("act_setup"), sem("dve_setup")
        parts = sem("parts")
        (hT_mm, u_mm, x1T_mm, v_mm, k_mm, q_mm, attT_mm, w1a_mm, w1b_mm, h2T_mm, y_mm, aks_mm, z_mm, r_mm,
         kk_mm, kv_mm) = map(sem, ("hT_mm u_mm x1T_mm v_mm k_mm q_mm attT_mm w1a_mm w1b_mm h2T_mm y_mm aks_mm "
                                   "z_mm r_mm kk_mm kv_mm").split())
        (hT_ok, x1T_ok, expk_ok, expq_ok, attT_ok, hida_ok, hidb_ok, h2T_ok, a_ok, tanh_ok, reluk_ok) = map(
            sem, "hT_ok x1T_ok expk_ok expq_ok attT_ok hida_ok hidb_ok h2T_ok a_ok tanh_ok reluk_ok".split())
        (n1_ok, ny_ok, n3_ok, k_ok, q_ok, wvm_ok, kvr_ok, den_ok, rden_ok, att_ok, z1_ok, x2_ok, mix_ok,
         prod_ok) = map(sem, ("n1_ok ny_ok n3_ok k_ok q_ok wvm_ok kvr_ok den_ok rden_ok att_ok z1_ok x2_ok mix_ok "
                              "prod_ok").split())
        stats_ok = {n: sem(f"stats_ok_{n}") for n in NORMS}
        mv_ok = {n: sem(f"mv_ok_{n}") for n in NORMS}
        s16_ok, kv_ok, xb_ok, diff_ok, ksq_ok, wvg_ok, out_ok = map(
            sem, "s16_ok kv_ok xb_ok diff_ok ksq_ok wvg_ok out_ok".split())
        vare_ok = {n: sem(f"vare_ok_{n}") for n in NORMS}
        rstd_ok = {n: sem(f"rstd_ok_{n}") for n in NORMS}

        x_dram = a["x"].rearrange("s (c p) d -> p (s c) d", p=128)
        out_dram = out.rearrange("s (c p) d -> s p c d", p=128)

        def chunked(bank):
            return bank[:, 0:NC * D].rearrange("p (c d) -> p c d", c=NC)

        def steps(eng, step):
            for t in range(STEPS_DEEP + 1):
                step(0, t)
            with eng.Fori(STEPS_DEEP // 2, S // 2 - 1) as j:
                for off in (1, 2):
                    step(j, off)
            for t in range(S - 1, S + STEPS_DEEP):
                step(0, t)

        def live(j, off):
            return not isinstance(j, int) or 0 <= off < S

        def need(eng, signal, count, most=S):
            if isinstance(count, int):
                count = min(count, most)
                if count <= 0:
                    return
            eng.wait_ge(signal, count)

        block = ctx.enter_context(nc.Block())

        @block.sync
        def _(sp):
            sp.dma_start(x_all[:, 0:NC, :], x_dram[:, 0:NC, :]).then_inc(x_in[0], 16)
            sp.dma_start(wmod[:, :], a["wmod"]).then_inc(wmod_loaded, 16)
            sp.dma_start(wk[:, :], a["Wk"]).then_inc(kq_loaded, 16)
            sp.dma_start(wq[:, :], a["Wq"]).then_inc(kq_loaded, 16)
            sp.dma_start(x_all[:, NC:2 * NC, :], x_dram[:, NC:2 * NC, :]).then_inc(x_in[1], 16)
            sp.dma_start(wv[:, :], a["Wv"]).then_inc(wvo_loaded, 16)
            sp.dma_start(wo[:, :], a["Wo"]).then_inc(wvo_loaded, 16)
            sp.dma_start(x_all[:, 2 * NC:4 * NC, :], x_dram[:, 2 * NC:4 * NC, :]).then_inc(x_in[2], 16)
            sp.dma_start(w1[:, :], a["W1"]).then_inc(w1_loaded, 16)
            sp.dma_start(w2[:, :, :], a["W2"].rearrange("(f p) d -> p f d", p=128)).then_inc(w2_loaded, 16)
            for i, name in enumerate(("W_r", "W_k", "W_v")):
                sp.dma_start(mix_w[:, i, :], a[name]).then_inc(mix_loaded, 16)
            sp.dma_start(x_all[:, 4 * NC:, :], x_dram[:, 4 * NC:, :]).then_inc(x_in[3], 16)
            sp.wait_ge(dve_setup, 8)
            sp.dma_start(scratch, mod_rows[:, :, :]).then_inc(rows_stored, 16)
            sp.wait_ge(rows_stored, 16)

            def load_bv(j, off):
                if not live(j, off):
                    return
                s, p = 2 * j + off, off % 2
                need(sp, kvr_ok, s - 1)
                sp.dma_start(bv_row[p][:, :], scratch[bass.ds(s, 1), BV_ROW, :].broadcast_to([128, D])).then_inc(bv_in[p], 16)

            def load_gm(j, off):
                if not live(j, off):
                    return
                s, p = 2 * j + off, off % 2
                need(sp, wvg_ok, s - 1)
                sp.dma_start(gm_rows[p][:, :, :],
                             scratch[bass.ds(s, 1), G_ROW:, :].broadcast_to([128, 3, D])).then_inc(gm_in[p], 16)

            def store(j, off):
                if not live(j, off):
                    return
                s = 2 * j + off
                need(sp, out_ok, s + 1)
                sp.dma_start(out_dram[bass.ds(s, 1), :, :, :].squeeze(0), out_sb[:, :, :]).then_inc(stored, 16)

            load_bv(0, 0)

            def step(j, off):
                load_bv(j, off + 1)
                store(j, off - 4)
                load_gm(j, off - 1)

            steps(sp, step)
            sp.wait_ge(stored, 16 * S)

        @block.scalar
        def _(act):
            act.dma_start(c_in[:, :], a["c"]).then_inc(c_loaded, 16)
            for i, name in enumerate(("g1", "beta1", "mu_r", "mu_k")):
                act.dma_start(vec_rows[i:i + 1, :], a[name].rearrange("(a d) -> a d", a=1)).then_inc(vec_loaded, 16)
            act.dma_start(vec_rows[4:8, :], a["b1"].rearrange("(a d) -> a d", d=128)).then_inc(vec_loaded, 16)
            for i, name in enumerate(("bk", "bq", "bo", "b2")):
                act.dma_start(bias3[:, i, :], a[name].rearrange("(a d) -> a d", a=1).broadcast_to([3, D])).then_inc(bias_loaded, 16)
            for i, name in enumerate(("g2", "beta2", "bv")):
                act.dma_start(row_in[:, i, :], a[name].rearrange("(a d) -> a d", a=1).broadcast_to([S, D])).then_inc(row_loaded, 16)
            act.wait_ge(pe_setup, 1)
            nc.scalar.activation(tanh_c[:, :], banks[0][:, 0:S], ACT.Tanh, scale=0.5).then_inc(act_setup, 1)
            act.wait_ge(pe_setup, 2)
            nc.scalar.activation(vec_cols[:, :], banks[5][:, 0:8], ACT.Copy).then_inc(act_setup, 1)
            act.wait_ge(pe_setup, 6)
            nc.scalar.activation(mix_wT[:, :], banks[7][:, 0:3 * D], ACT.Copy).then_inc(act_setup, 1)
            act.wait_ge(act_setup, 2)

            def col(i):
                return vec_cols[:, i:i + 1]
            g1_col, beta1_col = col(0), col(1)
            act.wait_ge(dve_setup, 3)

            def step(j, off):
                t = 2 * j + off
                sa, sb_, sd, sc = t, t - 1, t - 2, t - 3
                if live(j, off):
                    need(act, y_mm, sa - 1)
                    need(act, hT_mm, sa + 1)
                    nc.scalar.activation(hT[off % 2][:, :], banks[0][:, 0:L], ACT.Identity,
                                         scale=modT[:, bass.ds(CA * S + t, 1)],
                                         bias=modT[:, bass.ds(SA * S + t, 1)]).then_inc(hT_ok, 1)
                if live(j, off - 2):
                    need(act, x1T_mm, sd + 1)
                    nc.scalar.activation(x1T[:, :], banks[2][:, 0:L], ACT.Identity, scale=g1_col,
                                         bias=beta1_col).then_inc(x1T_ok, 1)
                if live(j, off):
                    need(act, k_mm, sa + 1)
                    nc.scalar.activation(exp_k[:, :, :], chunked(banks[4]), ACT.Exp, bias=neg1[:, :]).then_inc(expk_ok, 1)
                    need(act, q_mm, sa + 1)
                    nc.scalar.activation(exp_q[:, :], banks[5][:, 0:L], ACT.Exp, bias=neg1[:, :]).then_inc(expq_ok, 1)
                if live(j, off - 1):
                    need(act, attT_mm, sb_ + 1)
                    nc.scalar.activation(attT[:, :], banks[0][:, 0:L], ACT.Copy).then_inc(attT_ok, 1)
                if live(j, off - 2):
                    need(act, w1a_mm, sd + 1)
                    for f in range(FF):
                        if f == 2:
                            need(act, w1b_mm, sd + 1)
                        last = nc.scalar.activation(hid[:, f, :], banks[7 if f < 2 else 6][:, (f % 2) * L:(f % 2 + 1) * L],
                                                    ACT.Relu, bias=col(4 + f))
                        if f % 2:
                            last.then_inc(hidb_ok if f == 3 else hida_ok, 1)
                if live(j, off - 3):
                    need(act, h2T_mm, sc + 1)
                    nc.scalar.activation(h2T[:, 1:1 + L], banks[2][:, 0:L], ACT.Identity,
                                         scale=modT[:, bass.ds(CB * S + sc, 1)],
                                         bias=modT[:, bass.ds(SB * S + sc, 1)]).then_inc(h2T_ok, 1)
                if live(j, off):
                    need(act, aks_mm, sa + 1)
                    nc.scalar.activation(a_sb[:, :], banks[3][:, 0:D + 1], ACT.Copy).then_inc(a_ok, 1)
                if live(j, off - 3):
                    need(act, r_mm, sc + 1)
                    nc.scalar.activation(tanh_r[:, :, :], chunked(banks[5]), ACT.Tanh, scale=0.5).then_inc(tanh_ok, 1)
                    need(act, kk_mm, sc + 1)
                    nc.scalar.activation(relu_k[:, :], banks[7][:, 0:L], ACT.Relu).then_inc(reluk_ok, 1)

            steps(act, step)

        @block.gpsimd
        def _(pool):
            nc.gpsimd.memset(ident[:, :], 0.0).then_inc(const_pool, 1)
            nc.gpsimd.memset(headmask[:, :, :], 1.0).then_inc(const_pool, 1)
            pool.wait_ge(const_pool, 2)
            nc.gpsimd.affine_select(out=ident[:, :], in_=ident[:, :], compare_op=ALU.not_equal, fill=1.0, base=0,
                                    pattern=[[-1, 128]], channel_multiplier=1).then_inc(const_pool, 1)
            nc.gpsimd.affine_select(out=headmask[:, :, :], in_=headmask[:, :, :], compare_op=ALU.is_ge, fill=0.0,
                                    base=0, pattern=[[-DH, H], [0, DH]], channel_multiplier=1).then_inc(const_pool, 1)
            pool.wait_ge(const_pool, 4)
            nc.gpsimd.affine_select(out=headmask[:, :, :], in_=headmask[:, :, :], compare_op=ALU.is_ge, fill=0.0,
                                    base=DH - 1, pattern=[[DH, H], [0, DH]], channel_multiplier=-1).then_inc(const_pool, 1)
            pool.wait_ge(const_pool, 5)
            pool.wait_ge(const_dve, 6)

            def norm_scale(name, count):
                need(pool, mv_ok[name], count)
                nc.gpsimd.tensor_tensor(vare[name][:, :], mv[name][:, :, 1], eps[:, :], ALU.add).then_inc(vare_ok[name], 1)
                need(pool, vare_ok[name], count)
                nc.gpsimd.tensor_tensor(rstd[name][:, :], vare[name][:, :], power[:, :], ALU.pow).then_inc(rstd_ok[name], 1)

            norm_scale("n1", 1)

            def step(j, off):
                t = 2 * j + off
                sa, sb_, sd, sc, se = t, t - 1, t - 2, t - 3, t - 4
                if live(j, off - 4):
                    need(pool, stored, 16 * se, 16 * S)
                    need(pool, prod_ok, se + 1)
                    nc.gpsimd.tensor_tensor(out_sb[:, :, :], x2[off % 2][:, :, :], prod[:, :, :],
                                            ALU.add).then_inc(out_ok, 1)
                if live(j, off - 3):
                    norm_scale("n3", sc + 1)
                if live(j, off + 1):
                    norm_scale("n1", sa + 2)
                if live(j, off - 3):
                    need(pool, h2T_ok, sc + 1)
                    nc.gpsimd.tensor_tensor(diff[:, :], h2T[:, 1:1 + L], h2T[:, 0:L], ALU.subtract).then_inc(diff_ok, 1)
                if live(j, off - 1):
                    norm_scale("ny", sb_ + 1)
                if live(j, off):
                    need(pool, a_ok, sa + 1)
                    nc.gpsimd.tensor_tensor(kvs[:, D:D + H], headmask[:, :, 0], ksum[:, 0:1].broadcast_to([128, H]),
                                            ALU.mult).then_inc(s16_ok, 1)
                if live(j, off - 2):
                    need(pool, x2_ok, sd)
                    need(pool, gm_in[off % 2], 16 * (j + (off - 2) // 2 + 1), 16 * S)
                    nc.gpsimd.tensor_tensor(xb[:, :, :], x_all[:, bass.ds(NC * sd, NC), :],
                                            gm_rows[off % 2][:, GB_ROW - 1:GB_ROW, :].broadcast_to([128, NC, D]),
                                            ALU.add).then_inc(xb_ok, 1)
                if live(j, off):
                    need(pool, kvr_ok, sa + 1)
                    nc.gpsimd.tensor_tensor(kvs[:, 0:D], kv_raw[:, :], headmask[:, :, :].rearrange("p h d -> p (h d)"),
                                            ALU.mult).then_inc(kv_ok, 1)
                if live(j, off - 2):
                    norm_scale("z", sd + 1)
                if live(j, off - 3):
                    need(pool, reluk_ok, sc + 1)
                    nc.gpsimd.tensor_tensor(ksqT[:, :], relu_k[:, :], relu_k[:, :], ALU.mult).then_inc(ksq_ok, 1)
                    nc.gpsimd.tensor_tensor(wv_gate[:, :], mix_wT[:, 2 * D:3 * D], gm_rows[(off - 3) % 2][:, GATE_ROW - 1, :],
                                            ALU.mult).then_inc(wvg_ok, 1)

            pool.wait_ge(act_setup, 3)
            steps(pool, step)

        @block.vector
        def _(dve):
            nc.vector.memset(ones[:, :], 1.0).then_inc(const_dve, 1)
            nc.vector.memset(neg1[:, :], -1.0).then_inc(const_dve, 1)
            nc.vector.memset(ones3[:, :], 1.0).then_inc(const_dve, 1)
            nc.vector.memset(h2T[:, 0:1], 0.0).then_inc(const_dve, 1)
            nc.vector.memset(eps[:, :], EPS_LN).then_inc(const_dve, 1)
            nc.vector.memset(power[:, :], -0.5).then_inc(const_dve, 1)

            def norm_stats(name, source):
                for c in range(NC):
                    last = nc.vector.bn_stats(stats[name][:, c, :], source(c))
                last.then_inc(stats_ok[name], 1)

            def norm_mv(name):
                for c in range(NC):
                    last = nc.vector.bn_aggr(mv[name][:, c, :], stats[name][:, c, :])
                last.then_inc(mv_ok[name], 1)

            def normalise(name, dest, source, count, signal):
                need(dve, rstd_ok[name], count)
                for c in range(NC):
                    last = nc.vector.tensor_scalar(dest[:, c, :], source(c), mv[name][:, c, 0:1], rstd[name][:, c:c + 1],
                                                   ALU.subtract, ALU.mult)
                last.then_inc(signal, 1)

            def x_chunk(j, off):
                return lambda c: x_all[:, bass.ds(NC * (2 * j + off) + c, 1), :].squeeze(1)

            dve.wait_ge(x_in[0], 16)
            norm_stats("n1", x_chunk(0, 0))
            dve.wait_ge(stats_ok["n1"], 1)
            norm_mv("n1")
            dve.wait_ge(act_setup, 1)
            nc.vector.scalar_tensor_tensor(silu2[:, :], tanh_c[:, :], 1.0, banks[0][:, 0:S], ALU.add, ALU.mult).then_inc(dve_setup, 1)
            normalise("n1", n1[0], x_chunk(0, 0), 1, n1_ok)
            dve.wait_ge(dve_setup, 1)
            nc.vector.tensor_scalar(siluT[:, :], silu2[:, :], 0.5, None, ALU.mult).then_inc(dve_setup, 1)
            dve.wait_ge(bias_loaded, 64)
            dve.wait_ge(const_pool, 5)
            nc.vector.tensor_scalar(bias3[:, 0:2, :], bias3[:, 0:2, :], 1.0, None, ALU.add).then_inc(parts, 1)
            dve.wait_ge(parts, 1)
            nc.vector.tensor_copy(part_hi[:, :, :], bias3[:, :, :]).then_inc(parts, 1)
            dve.wait_ge(parts, 2)
            nc.vector.tensor_tensor(rest1[:, :, :], bias3[:, :, :], part_hi[:, :, :], ALU.subtract).then_inc(parts, 1)
            dve.wait_ge(parts, 3)
            nc.vector.tensor_copy(part_mid[:, :, :], rest1[:, :, :]).then_inc(parts, 1)
            dve.wait_ge(parts, 4)
            nc.vector.tensor_tensor(rest2[:, :, :], rest1[:, :, :], part_mid[:, :, :], ALU.subtract).then_inc(parts, 1)
            dve.wait_ge(parts, 5)
            nc.vector.tensor_copy(part_lo[:, :, :], rest2[:, :, :]).then_inc(parts, 1)
            nc.vector.tensor_scalar(pick1[:, :, :], part_hi[:, :, :], ident[0:3, 0:1], None, ALU.mult).then_inc(parts, 1)
            dve.wait_ge(parts, 7)
            nc.vector.scalar_tensor_tensor(pick2[:, :, :], part_mid[:, :, :], ident[0:3, 1:2], pick1[:, :, :], ALU.mult,
                                           ALU.add).then_inc(parts, 1)
            dve.wait_ge(parts, 8)
            nc.vector.scalar_tensor_tensor(bias_parts[:, :, :], part_lo[:, :, :], ident[0:3, 2:3], pick2[:, :, :], ALU.mult,
                                           ALU.add).then_inc(parts, 1)
            dve.wait_ge(pe_setup, 3)
            nc.vector.tensor_scalar(modT[:, 0:2 * S], banks[1][:, 0:2 * S], 1.0, None, ALU.add)
            nc.vector.tensor_copy(modT[:, 2 * S:4 * S], banks[1][:, 2 * S:4 * S]).then_inc(dve_setup, 1)

            def gate_rows():
                dve.wait_ge(pe_setup, 4)
                dve.wait_ge(row_loaded, 48)
                raw = banks[2][0:S, 0:2 * D].rearrange("p (k d) -> p k d", k=2)
                nc.vector.tensor_scalar(gate_sign[:, :, :], raw, 0.0, 2.0, ALU.is_ge, ALU.mult)
                nc.vector.tensor_scalar(gate_pos[:, :, :], raw, 0.25, None, ALU.max).then_inc(dve_setup, 1)
                dve.wait_ge(dve_setup, 4)
                nc.vector.scalar_tensor_tensor(gate_size[:, :, :], raw, -1.0, gate_pos[:, :, :], ALU.mult,
                                               ALU.max).then_inc(dve_setup, 1)
                dve.wait_ge(dve_setup, 5)
                nc.vector.scalar_tensor_tensor(gates[:, :, :], gate_sign[:, :, :], -1.0, gate_size[:, :, :], ALU.add,
                                               ALU.mult).then_inc(dve_setup, 1)
                dve.wait_ge(dve_setup, 6)
                nc.vector.tensor_tensor(mod_rows[:, G_ROW, :], gates[:, 0, :], row_in[:, 0, :], ALU.mult)
                nc.vector.tensor_tensor(mod_rows[:, GB_ROW, :], gates[:, 0, :], row_in[:, 1, :], ALU.mult)
                nc.vector.tensor_scalar(mod_rows[:, GATE_ROW, :], gates[:, 1, :], 0.5, None, ALU.mult).then_inc(dve_setup, 1)
                dve.wait_ge(pe_setup, 5)
                nc.vector.tensor_tensor(mod_rows[:, BV_ROW, :], banks[3][0:S, 0:D], row_in[:, 2, :], ALU.add).then_inc(dve_setup, 1)

            gate_rows()

            def step(j, off):
                t = 2 * j + off
                sa, sb_, sd, sc, se = t, t - 1, t - 2, t - 3, t - 4
                u = banks[1][:, 0:NC * (D + H)].rearrange("p (c e) -> p c e", c=NC)
                y = chunked(banks[1])
                z = chunked(banks[6])
                if live(j, off - 3):
                    need(dve, rstd_ok["z"], sc + 1)
                    for c in range(NC):
                        last = nc.vector.scalar_tensor_tensor(z1[:, c, :], z[:, c, :], mv["z"][:, c, 0:1],
                                                              gm_rows[(off - 3) % 2][:, G_ROW - 1, :], ALU.subtract, ALU.mult)
                    last.then_inc(z1_ok, 1)
                if live(j, off - 1):
                    need(dve, u_mm, sb_ + 1)
                    nc.vector.tensor_scalar(den[:, :, :], u[:, :, D:D + H], EPS_ATTN, None, ALU.add).then_inc(den_ok, 1)
                if live(j, off - 3):
                    need(dve, z1_ok, sc + 1)
                    need(dve, xb_ok, sc + 1)
                    need(dve, out_ok, sc - 1)
                    for c in range(NC):
                        last = nc.vector.scalar_tensor_tensor(x2[(off - 3) % 2][:, c, :], z1[:, c, :], rstd["z"][:, c:c + 1],
                                                              xb[:, c, :], ALU.mult, ALU.add)
                    last.then_inc(x2_ok, 1)
                if live(j, off - 1):
                    need(dve, den_ok, sb_ + 1)
                    nc.vector.reciprocal(rden[:, :, :], den[:, :, :]).then_inc(rden_ok, 1)
                    need(dve, rden_ok, sb_ + 1)
                    for c in range(NC):
                        last = nc.vector.tensor_tensor(att[:, c, :].rearrange("p (h d) -> p h d", h=H),
                                                       u[:, c, 0:D].rearrange("p (h d) -> p h d", h=H),
                                                       rden[:, c, :].unsqueeze(2).broadcast_to([128, H, DH]), ALU.mult)
                    last.then_inc(att_ok, 1)
                if live(j, off - 3):
                    need(dve, x2_ok, sc + 1)
                    norm_stats("n3", lambda c: x2[(off - 3) % 2][:, c, :])
                    need(dve, stats_ok["n3"], sc + 1)
                if live(j, off - 4):
                    need(dve, v_mm, se + 1)
                    need(dve, out_ok, se)
                    nc.vector.scalar_tensor_tensor(prod[:, :, :], tanh_r[:, :, :], 1.0, chunked(banks[3]), ALU.add,
                                                   ALU.mult).then_inc(prod_ok, 1)
                if live(j, off - 3):
                    norm_mv("n3")
                if live(j, off + 1):
                    if isinstance(j, int) and off < 4:
                        dve.wait_ge(x_in[(1, 2, 2, 3)[off]], 16)
                    norm_stats("n1", x_chunk(j, off + 1))
                    need(dve, stats_ok["n1"], sa + 2)
                if live(j, off):
                    need(dve, expk_ok, sa + 1)
                    nc.vector.scalar_tensor_tensor(k_sb[:, :, :], exp_k[:, :, :], 1.0, chunked(banks[4]), ALU.min,
                                                   ALU.max).then_inc(k_ok, 1)
                if live(j, off + 1):
                    norm_mv("n1")
                if live(j, off - 3):
                    need(dve, h2T_mm, sc)
                    normalise("n3", n3, lambda c: x2[(off - 3) % 2][:, c, :], sc + 1, n3_ok)
                if live(j, off):
                    need(dve, expq_ok, sa + 1)
                    nc.vector.scalar_tensor_tensor(qT[:, :], exp_q[:, :], 1.0, banks[5][:, 0:L], ALU.min,
                                                   ALU.max).then_inc(q_ok, 1)
                    need(dve, kv_mm, sa)
                    nc.vector.tensor_scalar(wv_mod[:, :], wv[:, :], modT[:, bass.ds(CA * S + t, 1)], None,
                                            ALU.mult).then_inc(wvm_ok, 1)
                if live(j, off - 1):
                    need(dve, y_mm, sb_ + 1)
                    norm_stats("ny", lambda c: y[:, c, :])
                    need(dve, stats_ok["ny"], sb_ + 1)
                if live(j, off + 1):
                    need(dve, aks_mm, sa)
                    normalise("n1", n1[(off + 1) % 2], x_chunk(j, off + 1), sa + 2, n1_ok)
                if live(j, off - 1):
                    norm_mv("ny")
                if live(j, off - 1):
                    normalise("ny", ny, lambda c: y[:, c, :], sb_ + 1, ny_ok)
                if live(j, off - 3):
                    need(dve, diff_ok, sc + 1)
                    nc.vector.scalar_tensor_tensor(xrT[:, :], diff[:, :], vec_cols[:, 2:3], h2T[:, 0:L], ALU.mult, ALU.add)
                    nc.vector.scalar_tensor_tensor(xkT[:, :], diff[:, :], vec_cols[:, 3:4], h2T[:, 0:L], ALU.mult,
                                                   ALU.add).then_inc(mix_ok, 1)
                if live(j, off - 2):
                    need(dve, z_mm, sd + 1)
                    norm_stats("z", lambda c: z[:, c, :])
                    need(dve, stats_ok["z"], sd + 1)
                if live(j, off):
                    need(dve, kv_mm, sa + 1)
                    need(dve, a_ok, sa + 1)
                    need(dve, bv_in[off % 2], 16 * (j + off // 2 + 1), 16 * S)
                    nc.vector.scalar_tensor_tensor(kv_raw[:, :], bv_row[off % 2][:, :], ksum[:, 0:1], banks[3][:, 0:D],
                                                   ALU.mult, ALU.add).then_inc(kvr_ok, 1)
                if live(j, off - 2):
                    norm_mv("z")

            dve.wait_ge(act_setup, 2)
            dve.wait_ge(wvo_loaded, 32)
            steps(dve, step)

        @block.tensor
        def _(pe):
            pe.wait_ge(const_pool, 5)
            pe.wait_ge(c_loaded, 16)
            nc.tensor.transpose(banks[0][:, 0:S], c_in[:, :], ident[0:S, 0:S]).then_inc(pe_setup, 1)
            pe.wait_ge(vec_loaded, 80)
            nc.tensor.transpose(banks[5][:, 0:8], vec_rows[:, :], ident[0:8, 0:8]).then_inc(pe_setup, 1)
            pe.wait_ge(dve_setup, 2)
            pe.wait_ge(wmod_loaded, 16)
            for i, chunk in enumerate((1, 4, 0, 3)):
                last = nc.tensor.matmul(banks[1][:, i * S:(i + 1) * S], wmod[:, chunk * D:(chunk + 1) * D], siluT[:, :],
                                        start=True, stop=True)
            last.then_inc(pe_setup, 1)
            for i, chunk in enumerate((2, 5)):
                last = nc.tensor.matmul(banks[2][0:S, i * D:(i + 1) * D], siluT[:, :], wmod[:, chunk * D:(chunk + 1) * D],
                                        start=True, stop=True)
            last.then_inc(pe_setup, 1)
            pe.wait_ge(dve_setup, 3)
            pe.wait_ge(wvo_loaded, 32)
            nc.tensor.matmul(banks[3][0:S, 0:D], modT[:, SA * S:(SA + 1) * S], wv[:, :], start=True, stop=True).then_inc(pe_setup, 1)
            pe.wait_ge(mix_loaded, 48)
            for i in range(3):
                last = nc.tensor.transpose(banks[7][:, i * D:(i + 1) * D], mix_w[:, i, :], ident[:, :])
            last.then_inc(pe_setup, 1)
            pe.wait_ge(kq_loaded, 32)
            pe.wait_ge(w1_loaded, 16)
            pe.wait_ge(w2_loaded, 16)
            pe.wait_ge(parts, 9)
            pe.wait_ge(act_setup, 3)
            wrT, wkT = mix_wT[:, 0:D], mix_wT[:, D:2 * D]

            def transpose_in(bank, tile, signal):
                for c in range(NC):
                    last = nc.tensor.transpose(bank[:, c * 128:(c + 1) * 128], tile[:, c, :], ident[:, :])
                last.then_inc(signal, 1)

            def bias_into(bank, i):
                nc.tensor.matmul(chunked(bank), ones3[:, 0:128], bias_parts[:, i:i + 1, :].broadcast_to([3, NC, D]),
                                 start=True, stop=False)

            def residual_into(bank, tileT, c):
                return nc.tensor.matmul(bank[:, c * D:(c + 1) * D], tileT[:, c * 128:(c + 1) * 128], ident[:, :],
                                        start=False, stop=False, is_transpose=RES_TRANSPOSE)

            def feed_forward_out(f0, f1):
                for f in range(f0, f1):
                    for c in range(NC):
                        last = nc.tensor.matmul(banks[6][:, c * D:(c + 1) * D], hid[:, f, c * 128:(c + 1) * 128], w2[:, f, :],
                                                start=False, stop=(f == FF - 1 and c == NC - 1))
                return last

            def step(j, off):
                t = 2 * j + off
                sa, sb_, sd, sc, se = t, t - 1, t - 2, t - 3, t - 4
                if live(j, off):
                    need(pe, n1_ok, sa + 1)
                    need(pe, attT_ok, sa - 1)
                    transpose_in(banks[0], n1[off % 2], hT_mm)
                if live(j, off - 1):
                    need(pe, q_ok, sb_ + 1)
                    need(pe, s16_ok, sb_ + 1)
                    need(pe, kv_ok, sb_ + 1)
                    need(pe, ny_ok, sb_)
                    for c in range(NC):
                        last = nc.tensor.matmul(banks[1][:, c * (D + H):(c + 1) * (D + H)], qT[:, c * 128:(c + 1) * 128],
                                                kvs[:, :], start=True, stop=True)
                    last.then_inc(u_mm, 1)
                if live(j, off - 2):
                    need(pe, ny_ok, sd + 1)
                    need(pe, h2T_ok, sd - 1)
                    transpose_in(banks[2], ny, x1T_mm)
                if live(j, off - 4):
                    need(pe, ksq_ok, se + 1)
                    need(pe, wvg_ok, se + 1)
                    need(pe, kvr_ok, se + 4)
                    for c in range(NC):
                        last = nc.tensor.matmul(banks[3][:, c * D:(c + 1) * D], ksqT[:, c * 128:(c + 1) * 128], wv_gate[:, :],
                                                start=True, stop=True)
                    last.then_inc(v_mm, 1)
                if live(j, off):
                    need(pe, hT_ok, sa + 1)
                    need(pe, k_ok, sa)
                    bias_into(banks[4], 0)
                    for c in range(NC):
                        last = nc.tensor.matmul(banks[4][:, c * D:(c + 1) * D], hT[off % 2][:, c * 128:(c + 1) * 128],
                                                wk[:, :], start=False, stop=(c == NC - 1))
                    last.then_inc(k_mm, 1)
                    need(pe, q_ok, sa)
                    need(pe, tanh_ok, sa - 3)
                    nc.tensor.matmul(banks[5][:, 0:L], bias_parts[:, 1, :], ones3[:, :], start=True, stop=False)
                    nc.tensor.matmul(banks[5][:, 0:L], wq[:, :], hT[off % 2][:, :], start=False, stop=True).then_inc(q_mm, 1)
                if live(j, off - 1):
                    need(pe, att_ok, sb_ + 1)
                    need(pe, hT_ok, sb_ + 2)
                    transpose_in(banks[0], att, attT_mm)
                if live(j, off - 2):
                    need(pe, x1T_ok, sd + 1)
                    need(pe, hida_ok, sd)
                    need(pe, reluk_ok, sd - 1)
                    for f in range(2):
                        last = nc.tensor.matmul(banks[7][:, f * L:(f + 1) * L], w1[:, f * 128:(f + 1) * 128], x1T[:, :],
                                                start=True, stop=True)
                    last.then_inc(w1a_mm, 1)
                    need(pe, z1_ok, sd)
                    for f in range(2):
                        last = nc.tensor.matmul(banks[6][:, f * L:(f + 1) * L], w1[:, (2 + f) * 128:(3 + f) * 128],
                                                x1T[:, :], start=True, stop=True)
                    last.then_inc(w1b_mm, 1)
                if live(j, off - 3):
                    need(pe, n3_ok, sc + 1)
                    need(pe, x1T_ok, sc + 2)
                    transpose_in(banks[2], n3, h2T_mm)
                if live(j, off - 1):
                    need(pe, attT_ok, sb_ + 1)
                    bias_into(banks[1], 2)
                    for c in range(NC):
                        residual_into(banks[1], hT[(off - 1) % 2], c)
                        last = nc.tensor.matmul(banks[1][:, c * D:(c + 1) * D], attT[:, c * 128:(c + 1) * 128], wo[:, :],
                                                start=False, stop=(c == NC - 1))
                    last.then_inc(y_mm, 1)
                if live(j, off):
                    need(pe, k_ok, sa + 1)
                    if live(j, off - 4):
                        need(pe, prod_ok, se + 1)
                    else:
                        need(pe, kvr_ok, sa)
                    for c in range(NC):
                        nc.tensor.matmul(banks[3][:, 0:D], n1[off % 2][:, c, :], k_sb[:, c, :], start=(c == 0),
                                         stop=(c == NC - 1))
                    for c in range(NC):
                        last = nc.tensor.matmul(banks[3][:, D:D + 1], k_sb[:, c, :], ones[:, :], start=(c == 0),
                                                stop=(c == NC - 1))
                    last.then_inc(aks_mm, 1)
                if live(j, off - 2):
                    need(pe, hidb_ok, sd + 1)
                    bias_into(banks[6], 3)
                    for c in range(NC):
                        residual_into(banks[6], x1T, c)
                    feed_forward_out(0, 2)
                if live(j, off):
                    need(pe, a_ok, sa + 1)
                    need(pe, wvm_ok, sa + 1)
                    nc.tensor.matmul(banks[3][:, 0:D], a_sb[:, 0:D], wv_mod[:, :], start=True, stop=True).then_inc(kv_mm, 1)
                if live(j, off - 2):
                    feed_forward_out(2, FF).then_inc(z_mm, 1)
                if live(j, off - 3):
                    need(pe, mix_ok, sc + 1)
                    need(pe, q_ok, sc + 4)
                    for c in range(NC):
                        last = nc.tensor.matmul(banks[5][:, c * D:(c + 1) * D], xrT[:, c * 128:(c + 1) * 128], wrT,
                                                start=True, stop=True)
                    last.then_inc(r_mm, 1)
                    need(pe, hida_ok, sc + 2)
                    nc.tensor.matmul(banks[7][:, 0:L], wkT, xkT[:, :], start=True, stop=True).then_inc(kk_mm, 1)

            steps(pe, step)


RES_TRANSPOSE = True

_NAMES = ("x", "Wq", "bq", "Wk", "bk", "Wv", "bv", "Wo", "bo", "W1", "b1", "W2", "b2", "g1", "beta1", "g2", "beta2")
_INS = {f"L0_attn_{n}": n for n in _NAMES}
_INS |= {f"L0_ffn_{n}": n for n in ("W_r", "W_k", "W_v", "mu_r", "mu_k")}
_INS |= {"L0_c": "c", "L0_wmod": "wmod"}


def kernel(**inputs):
    import concourse.bacc as bacc
    from concourse.bass_utils import run_bass_kernel_spmd

    nc = bacc.Bacc("TRN2", target_bir_lowering=False, num_devices=1)
    arrays, aps = {}, {}
    for name, short in _INS.items():
        arr = np.ascontiguousarray(inputs[name])
        arrays[f"in_{name}"] = arr
        aps[short] = nc.dram_tensor(f"in_{name}", arr.shape, mybir.dt.from_np(arr.dtype), kind="ExternalInput").ap()
    out = nc.dram_tensor("out", (S, L, D), F32, kind="ExternalOutput").ap()
    scratch = nc.dram_tensor("mod_rows_dram", (S, 4, D), F32, kind="Internal").ap()
    build(nc, aps, out, scratch)
    r = run_bass_kernel_spmd(nc, [arrays], core_ids=[0])
    return r.results[0]["out"]
```

```python
from contextlib import ExitStack

import numpy as np

import concourse.bass as bass
from concourse import mybir

F32 = mybir.dt.float32
BF16 = mybir.dt.bfloat16
ALU = mybir.AluOpType
ACT = mybir.ActivationFunctionType

S, L, D = 16, 256, 128
NC = L // 128
H, DH = 16, 8
FF = 4
EPS_ATTN = 1e-6
EPS_LN = 1e-5
WARM = 7
STEPS_DEEP = 4
CA, CB, SA, SB, MOVE, KEEP, FIRST, KINDS = 0, 1, 2, 3, 4, 6, 8, 10
G_ROW, GB_ROW, GATE_ROW = range(3)


def build(nc, a, out, scratch):
    with ExitStack() as ctx:
        def sb(name, shape, dt=F32):
            return ctx.enter_context(nc.sbuf_tensor(name, shape, dt))

        def sem(name):
            return ctx.enter_context(nc.semaphore(name))

        banks = [ctx.enter_context(nc.psum_tensor(f"bank{i}", [128, 512], F32)) for i in range(8)]

        kqvo = sb("kqvo", [128, 4, D])
        wk, wq, wv, wo = (kqvo[:, i, :] for i in range(4))
        w12 = sb("w12", [128, 2, FF * 128])
        w1, w2 = w12[:, 0, :], w12[:, 1, :].rearrange("p (f d) -> p f d", f=FF)
        mix_w = sb("mix_w", [128, 3, D])
        wrT, wkT, wvT = (mix_w[:, i, :] for i in range(3))
        cols = sb("cols", [128, S + 8])
        wmod = sb("wmod", [128, 6 * D])
        ident = sb("ident", [128, 128])
        ones = sb("ones", [128, 1])
        headmask = sb("headmask", [128, H, DH])
        power = sb("power", [128, NC])
        eps = sb("eps", [128, NC])
        ones3 = sb("ones3", [3, L], BF16)
        neg1 = sb("neg1", [128, 1])
        table_load = sb("table_load", [128, 1])
        tanh_c = sb("tanh_c", [128, S])
        silu2 = sb("silu2", [128, S])
        siluT = sb("siluT", [128, S])
        modT = sb("modT", [128, KINDS, S])
        row_in = sb("row_in", [S, 3, D])
        gate_sign = sb("gate_sign", [S, 2, D])
        gate_pos = sb("gate_pos", [S, 2, D])
        gate_size = sb("gate_size", [S, 2, D])
        gates = sb("gates", [S, 2, D])
        mod_rows = sb("mod_rows", [S, 3, D])
        bv_rows = sb("bv_rows", [S, D])
        bias3 = sb("bias3", [3, 4, D])
        part_mask = sb("part_mask", [3, 2])
        high = [sb(f"high{i}", [3, 4, D], BF16) for i in range(2)]
        rest = sb("rest", [3, 4, D])
        bias_parts = sb("bias_parts", [3, 4, D], BF16)
        x_all = sb("x_all", [128, S * NC, D])
        bv_row = [sb(f"bv_row{p}", [128, D]) for p in range(2)]
        gm_rows = [sb(f"gm_rows{p}", [128, 3, D]) for p in range(2)]
        n1 = [sb(f"n1_{p}", [128, NC, D]) for p in range(2)]
        hT = [sb(f"hT{p}", [128, L]) for p in range(2)]
        exp_k = sb("exp_k", [128, NC, D])
        k_sb = sb("k_sb", [128, NC, D])
        exp_q = sb("exp_q", [128, L])
        qT = sb("qT", [128, L])
        a_sb = sb("a_sb", [128, D + 1])
        wv_mod = sb("wv_mod", [128, D])
        ksum = a_sb[:, D:D + 1]
        kv_raw = sb("kv_raw", [128, D])
        kvs = sb("kvs", [128, D + H])
        den = sb("den", [128, NC, H])
        rden = sb("rden", [128, NC, H])
        att = sb("att", [128, NC, D])
        attT = sb("attT", [128, L])
        ny = sb("ny", [128, NC, D])
        x1T = sb("x1T", [128, L])
        hid = sb("hid", [128, FF, L])
        z1 = sb("z1", [128, NC, D])
        xb = sb("xb", [128, NC, D])
        x2 = [sb(f"x2_{p}", [128, NC, D]) for p in range(2)]
        n3 = sb("n3", [128, NC, D])
        keepT = sb("keepT", [128, 2, L])
        mixT = sb("mixT", [128, 2, L])
        tanh_r = sb("tanh_r", [128, NC, D])
        relu_k = sb("relu_k", [128, L])
        ksqT = sb("ksqT", [128, L])
        wv_gate = sb("wv_gate", [128, D])
        prod = sb("prod", [128, NC, D])
        out_sb = sb("out_sb", [128, NC, D])
        NORMS = ("n1", "ny", "z", "n3")
        stats = {n: sb(f"stats_{n}", [128, NC, 6]) for n in NORMS}
        mv = {n: sb(f"mv_{n}", [128, NC, 2]) for n in NORMS}
        vare = {n: sb(f"vare_{n}", [128, NC]) for n in NORMS}
        rstd = {n: sb(f"rstd_{n}", [128, NC]) for n in NORMS}

        x_in = [sem(f"x_in{i}") for i in range(3)]
        cols_loaded, wmod_loaded, kq_loaded = map(sem, ("cols_loaded", "wmod_loaded", "kq_loaded"))
        wvo_loaded, w12_loaded, mix_loaded = map(sem, ("wvo_loaded", "w12_loaded", "mix_loaded"))
        row_loaded, bias_loaded, bv_stored, rows_stored = map(sem, ("row_loaded", "bias_loaded", "bv_stored", "rows_stored"))
        bv_in = [sem(f"bv_in{p}") for p in range(2)]
        gm_in = [sem(f"gm_in{p}") for p in range(2)]
        stored = sem("stored")
        const_pool, const_dve = sem("const_pool"), sem("const_dve")
        tanh_c_ok, silu_ok = sem("tanh_c_ok"), sem("silu_ok")
        cols_mm, gates_mm, bv_mm = sem("cols_mm"), sem("gates_mm"), sem("bv_mm")
        parts, cols_ok, bv_ok = sem("parts"), sem("cols_ok"), sem("bv_ok")
        gate_ok, shift_cols = sem("gate_ok"), sem("shift_cols")
        (hT_mm, u_mm, x1T_mm, v_mm, k_mm, q_mm, attT_mm, w1a_mm, w1b_mm, h2T_mm, y_mm, aks_mm, z_mm, r_mm,
         kk_mm, kv_mm) = map(sem, ("hT_mm u_mm x1T_mm v_mm k_mm q_mm attT_mm w1a_mm w1b_mm h2T_mm y_mm aks_mm "
                                   "z_mm r_mm kk_mm kv_mm").split())
        (hT_ok, x1T_ok, expk_ok, expq_ok, attT_ok, hida_ok, hidb_ok, keep_ok, a_ok, tanh_ok, reluk_ok, ksq_ok) = map(
            sem, ("hT_ok x1T_ok expk_ok expq_ok attT_ok hida_ok hidb_ok keep_ok a_ok tanh_ok reluk_ok "
                 "ksq_ok").split())
        (n1_ok, ny_ok, n3_ok, k_ok, q_ok, wvm_ok, kvr_ok, den_ok, rden_ok, att_ok, z1_ok, x2_ok, mix_ok,
         prod_ok) = map(sem, ("n1_ok ny_ok n3_ok k_ok q_ok wvm_ok kvr_ok den_ok rden_ok att_ok z1_ok x2_ok mix_ok "
                              "prod_ok").split())
        stats_ok = {n: sem(f"stats_ok_{n}") for n in NORMS}
        mv_ok = {n: sem(f"mv_ok_{n}") for n in NORMS}
        s16_ok, kv_ok, xb_ok, wvg_ok, out_ok = map(sem, "s16_ok kv_ok xb_ok wvg_ok out_ok".split())
        vare_ok = {n: sem(f"vare_ok_{n}") for n in NORMS}
        rstd_ok = {n: sem(f"rstd_ok_{n}") for n in NORMS}

        x_dram = a["x"].rearrange("s (c p) d -> p (s c) d", p=128)
        out_dram = out.rearrange("s (c p) d -> s p c d", p=128)

        def chunked(bank):
            return bank[:, 0:NC * D].rearrange("p (c d) -> p c d", c=NC)

        def steps(eng, step):
            for t in range(STEPS_DEEP + 1):
                step(0, t)
            with eng.Fori(STEPS_DEEP // 2, S // 2 - 1) as j:
                for off in (1, 2):
                    step(j, off)
            for t in range(S - 1, S + STEPS_DEEP):
                step(0, t)

        def live(j, off):
            return not isinstance(j, int) or 0 <= off < S

        def draining(j, off):
            return isinstance(j, int) and off >= S

        def hidden_bank(j, off):
            return banks[3] if draining(j, off) else banks[6]

        def need(eng, signal, count, most=S):
            if isinstance(count, int):
                count = min(count, most)
                if count <= 0:
                    return
            eng.wait_ge(signal, count)

        block = ctx.enter_context(nc.Block())

        @block.sync
        def _(sp):
            sp.dma_start(x_all[:, 0:NC, :], x_dram[:, 0:NC, :]).then_inc(x_in[0], 16)
            sp.dma_start(kqvo[:, 0:2, :], a["kqvo"][:, 0:2, :]).then_inc(kq_loaded, 16)
            sp.dma_start(kqvo[:, 2:4, :], a["kqvo"][:, 2:4, :]).then_inc(wvo_loaded, 16)
            sp.dma_start(x_all[:, NC:4 * NC, :], x_dram[:, NC:4 * NC, :]).then_inc(x_in[1], 16)
            sp.dma_start(w12[:, :, :], a["w12"]).then_inc(w12_loaded, 16)
            sp.dma_start(x_all[:, 4 * NC:, :], x_dram[:, 4 * NC:, :]).then_inc(x_in[2], 16)
            sp.wait_ge(bv_ok, 1)
            sp.dma_start(scratch["bv"], bv_rows[:, :]).then_inc(bv_stored, 16)
            sp.wait_ge(bv_stored, 16)

            def load_bv(j, off):
                if not live(j, off):
                    return
                s, p = 2 * j + off, off % 2
                need(sp, kvr_ok, s - 1)
                sp.dma_start(bv_row[p][:, :], scratch["bv"][bass.ds(s, 1), :].broadcast_to([128, D])).then_inc(bv_in[p], 16)

            def load_gm(j, off):
                if not live(j, off):
                    return
                s, p = 2 * j + off, off % 2
                need(sp, wvg_ok, s - 1)
                sp.dma_start(gm_rows[p][:, :, :],
                             scratch["rows"][bass.ds(s, 1), :, :].broadcast_to([128, 3, D])).then_inc(gm_in[p], 16)

            def store(j, off):
                if not live(j, off):
                    return
                s = 2 * j + off
                need(sp, out_ok, s + 1)
                sp.dma_start(out_dram[bass.ds(s, 1), :, :, :].squeeze(0), out_sb[:, :, :]).then_inc(stored, 16)

            load_bv(0, 0)
            load_bv(0, 1)
            sp.wait_ge(gate_ok, 4)
            sp.dma_start(scratch["rows"], mod_rows[:, :, :]).then_inc(rows_stored, 16)
            sp.wait_ge(rows_stored, 16)

            def step(j, off):
                if not isinstance(j, int) or off > 0:
                    load_bv(j, off + 1)
                load_gm(j, off - 2)
                store(j, off - 4)

            steps(sp, step)
            sp.wait_ge(stored, 16 * S)

        @block.scalar
        def _(act):
            act.dma_start(cols[:, :], a["cols"]).then_inc(cols_loaded, 16)
            act.dma_start(wmod[:, :], a["wmod"]).then_inc(wmod_loaded, 16)
            act.dma_start(bias3[:, :, :], a["bias"].rearrange("(a k) d -> a k d", a=1).broadcast_to([3, 4, D])).then_inc(bias_loaded, 16)
            act.wait_ge(const_dve, 2)
            nc.scalar.activation(table_load[:, :], neg1[:, :], ACT.Tanh)
            act.wait_ge(cols_loaded, 16)
            nc.scalar.activation(tanh_c[:, :], cols[:, 0:S], ACT.Tanh, scale=0.5).then_inc(tanh_c_ok, 1)
            act.dma_start(mix_w[:, :, :], a["mix_w"]).then_inc(mix_loaded, 16)

            def col(i):
                return cols[:, S + i:S + i + 1]
            g1_col, beta1_col = col(0), col(1)
            act.wait_ge(cols_ok, 1)

            def mod_col(kind, s):
                return modT[:, kind, bass.ds(s, 1)]

            def step(j, off):
                t = 2 * j + off
                sa, sb_, sd, sc = t, t - 1, t - 2, t - 4
                if live(j, off):
                    need(act, y_mm, sa - 1)
                    need(act, hT_mm, sa + 1)
                    nc.scalar.activation(hT[off % 2][:, :], banks[0][:, 0:L], ACT.Identity, scale=mod_col(CA, sa),
                                         bias=mod_col(SA, sa)).then_inc(hT_ok, 1)
                if live(j, off - 2):
                    need(act, x1T_mm, sd + 1)
                    nc.scalar.activation(x1T[:, :], banks[7][:, 0:L], ACT.Identity, scale=g1_col,
                                         bias=beta1_col).then_inc(x1T_ok, 1)
                if live(j, off - 4):
                    need(act, mix_ok, sc)
                    need(act, h2T_mm, sc + 1)
                    if isinstance(j, int) and sc == 0:
                        act.wait_ge(shift_cols, 2)
                    nc.scalar.activation(keepT[:, :, 0:1], modT[:, FIRST:FIRST + 2, bass.ds(sc, 1)], ACT.Copy)
                    for i in range(2):
                        last = nc.scalar.activation(keepT[:, i, 1:L], banks[2][:, 0:L - 1], ACT.Identity,
                                                    scale=mod_col(KEEP + i, sc), bias=mod_col(SB, sc))
                    last.then_inc(keep_ok, 1)
                if live(j, off):
                    need(act, k_mm, sa + 1)
                    nc.scalar.activation(exp_k[:, :, :], chunked(banks[4]), ACT.Exp, bias=neg1[:, :]).then_inc(expk_ok, 1)
                    need(act, q_mm, sa + 1)
                    nc.scalar.activation(exp_q[:, :], banks[5][:, 0:L], ACT.Exp, bias=neg1[:, :]).then_inc(expq_ok, 1)
                    act.wait_ge(wvo_loaded, 16)
                    need(act, kv_mm, sa)
                    nc.scalar.activation(wv_mod[:, :], wv, ACT.Copy, scale=mod_col(CA, sa)).then_inc(wvm_ok, 1)
                if live(j, off - 2):
                    need(act, w1a_mm, sd + 1)
                    for f in range(2):
                        last = nc.scalar.activation(hid[:, f, :], banks[7][:, f * L:(f + 1) * L], ACT.Relu, bias=col(4 + f))
                    last.then_inc(hida_ok, 1)
                if live(j, off - 1):
                    need(act, attT_mm, sb_ + 1)
                    nc.scalar.activation(attT[:, :], banks[0][:, 0:L], ACT.Copy).then_inc(attT_ok, 1)
                if live(j, off - 2):
                    need(act, w1b_mm, sd + 1)
                    for f in range(2, FF):
                        last = nc.scalar.activation(hid[:, f, :], hidden_bank(j, off)[:, (f - 2) * L:(f - 1) * L], ACT.Relu,
                                                    bias=col(4 + f))
                    last.then_inc(hidb_ok, 1)
                if live(j, off):
                    need(act, aks_mm, sa + 1)
                    nc.scalar.activation(a_sb[:, :], banks[3][:, 0:D + 1], ACT.Copy).then_inc(a_ok, 1)
                if live(j, off - 4):
                    need(act, kk_mm, sc + 1)
                    nc.scalar.activation(relu_k[:, :], banks[2][:, 0:L], ACT.Relu).then_inc(reluk_ok, 1)
                    need(act, reluk_ok, sc + 1)
                    nc.scalar.activation(ksqT[:, :], relu_k[:, :], ACT.Square).then_inc(ksq_ok, 1)
                    need(act, prod_ok, sc)
                    need(act, r_mm, sc + 1)
                    nc.scalar.activation(tanh_r[:, :, :], chunked(banks[4]), ACT.Tanh, scale=0.5).then_inc(tanh_ok, 1)

            steps(act, step)

        @block.gpsimd
        def _(pool):
            nc.gpsimd.memset(ident[:, :], 0.0).then_inc(const_pool, 1)
            nc.gpsimd.memset(headmask[:, :, :], 1.0).then_inc(const_pool, 1)
            pool.wait_ge(const_pool, 2)
            nc.gpsimd.affine_select(out=ident[:, :], in_=ident[:, :], compare_op=ALU.not_equal, fill=1.0, base=0,
                                    pattern=[[-1, 128]], channel_multiplier=1).then_inc(const_pool, 1)
            nc.gpsimd.affine_select(out=headmask[:, :, :], in_=headmask[:, :, :], compare_op=ALU.is_ge, fill=0.0,
                                    base=0, pattern=[[-DH, H], [0, DH]], channel_multiplier=1).then_inc(const_pool, 1)
            pool.wait_ge(const_pool, 4)
            nc.gpsimd.affine_select(out=headmask[:, :, :], in_=headmask[:, :, :], compare_op=ALU.is_ge, fill=0.0,
                                    base=DH - 1, pattern=[[DH, H], [0, DH]], channel_multiplier=-1).then_inc(const_pool, 1)
            pool.dma_start(row_in[:, :, :], a["rows"].rearrange("(a k) d -> a k d", a=1).broadcast_to([S, 3, D])).then_inc(row_loaded, 16)
            pool.wait_ge(const_dve, 5)

            def norm_scale(name, count):
                need(pool, mv_ok[name], count)
                nc.gpsimd.tensor_tensor(vare[name][:, :], mv[name][:, :, 1], eps[:, :], ALU.add).then_inc(vare_ok[name], 1)
                need(pool, vare_ok[name], count)
                nc.gpsimd.tensor_tensor(rstd[name][:, :], vare[name][:, :], power[:, :], ALU.pow).then_inc(rstd_ok[name], 1)

            norm_scale("n1", 1)

            def step(j, off):
                t = 2 * j + off
                sa, sb_, sd, sp_, sc = t, t - 1, t - 2, t - 3, t - 4
                if live(j, off + 1):
                    norm_scale("n1", sa + 2)
                if live(j, off - 4):
                    need(pool, v_mm, sc)
                    if isinstance(j, int) and sc == 0:
                        pool.wait_ge(mix_loaded, 16)
                    nc.gpsimd.tensor_tensor(wv_gate[:, :], wvT, gm_rows[off % 2][:, GATE_ROW, :],
                                            ALU.mult).then_inc(wvg_ok, 1)
                if live(j, off - 3):
                    norm_scale("n3", sp_ + 1)
                if live(j, off):
                    need(pool, a_ok, sa + 1)
                    nc.gpsimd.tensor_tensor(kvs[:, D:D + H], headmask[:, :, 0], ksum.broadcast_to([128, H]),
                                            ALU.mult).then_inc(s16_ok, 1)
                if live(j, off - 1):
                    norm_scale("ny", sb_ + 1)
                if live(j, off):
                    need(pool, kvr_ok, sa + 1)
                    nc.gpsimd.tensor_tensor(kvs[:, 0:D], kv_raw[:, :], headmask[:, :, :].rearrange("p h d -> p (h d)"),
                                            ALU.mult).then_inc(kv_ok, 1)
                if live(j, off - 2):
                    need(pool, x2_ok, sd)
                    need(pool, gm_in[off % 2], 16 * (j + (off - 2) // 2 + 1), 16 * S)
                    nc.gpsimd.tensor_tensor(xb[:, :, :], x_all[:, bass.ds(NC * sd, NC), :],
                                            gm_rows[off % 2][:, GB_ROW:GB_ROW + 1, :].broadcast_to([128, NC, D]),
                                            ALU.add).then_inc(xb_ok, 1)
                    norm_scale("z", sd + 1)
                if live(j, off - 4):
                    need(pool, stored, 16 * sc, 16 * S)
                    need(pool, prod_ok, sc + 1)
                    nc.gpsimd.tensor_tensor(out_sb[:, :, :], x2[off % 2][:, :, :], prod[:, :, :],
                                            ALU.add).then_inc(out_ok, 1)

            steps(pool, step)

        @block.vector
        def _(dve):
            nc.vector.memset(ones[:, :], 1.0).then_inc(const_dve, 1)
            nc.vector.memset(neg1[:, :], -1.0).then_inc(const_dve, 1)
            nc.vector.memset(ones3[:, :], 1.0).then_inc(const_dve, 1)
            nc.vector.memset(eps[:, :], EPS_LN).then_inc(const_dve, 1)
            nc.vector.memset(power[:, :], -0.5).then_inc(const_dve, 1)

            def norm_stats(name, source):
                for c in range(NC):
                    ins = nc.vector.bn_stats(stats[name][:, c, :], source(c))
                ins.then_inc(stats_ok[name], 1)

            def norm_mv(name, count=None):
                if count is not None:
                    dve.wait_ge(const_dve, 1)
                    need(dve, stats_ok[name], count)
                for c in range(NC):
                    ins = nc.vector.bn_aggr(mv[name][:, c, :], stats[name][:, c, :])
                ins.then_inc(mv_ok[name], 1)

            def normalise(name, dest, source, count, signal):
                need(dve, rstd_ok[name], count)
                for c in range(NC):
                    last = nc.vector.tensor_scalar(dest[:, c, :], source(c), mv[name][:, c, 0:1], rstd[name][:, c:c + 1],
                                                   ALU.subtract, ALU.mult)
                last.then_inc(signal, 1)

            def gate_rows():
                dve.wait_ge(gates_mm, 1)
                raw = banks[2][0:S, 0:2 * D].rearrange("p (k d) -> p k d", k=2)
                nc.vector.tensor_scalar(gate_sign[:, :, :], raw, 0.0, 2.0, ALU.is_ge, ALU.mult)
                nc.vector.tensor_scalar(gate_pos[:, :, :], raw, 0.25, None, ALU.max).then_inc(gate_ok, 1)
                dve.wait_ge(gate_ok, 1)
                nc.vector.scalar_tensor_tensor(gate_size[:, :, :], raw, -1.0, gate_pos[:, :, :], ALU.mult,
                                               ALU.max).then_inc(gate_ok, 1)
                dve.wait_ge(gate_ok, 2)
                nc.vector.scalar_tensor_tensor(gates[:, :, :], gate_sign[:, :, :], -1.0, gate_size[:, :, :], ALU.add,
                                               ALU.mult).then_inc(gate_ok, 1)
                dve.wait_ge(gate_ok, 3)
                nc.vector.tensor_tensor(mod_rows[:, G_ROW, :], gates[:, 0, :], row_in[:, 0, :], ALU.mult)
                nc.vector.tensor_tensor(mod_rows[:, GB_ROW, :], gates[:, 0, :], row_in[:, 1, :], ALU.mult)
                nc.vector.tensor_scalar(mod_rows[:, GATE_ROW, :], gates[:, 1, :], 0.5, None, ALU.mult).then_inc(gate_ok, 1)

            def x_chunk(j, off):
                return lambda c: x_all[:, bass.ds(NC * (2 * j + off) + c, 1), :].squeeze(1)

            dve.wait_ge(x_in[0], 16)
            norm_stats("n1", x_chunk(0, 0))
            norm_mv("n1", 1)
            dve.wait_ge(tanh_c_ok, 1)
            nc.vector.scalar_tensor_tensor(silu2[:, :], tanh_c[:, :], 1.0, cols[:, 0:S], ALU.add, ALU.mult).then_inc(silu_ok, 1)
            dve.wait_ge(silu_ok, 1)
            nc.vector.tensor_scalar(siluT[:, :], silu2[:, :], 0.5, None, ALU.mult).then_inc(silu_ok, 1)

            dve.wait_ge(const_pool, 3)
            nc.vector.tensor_scalar(part_mask[:, 0:1], ident[0:3, 0:1], 1.0, None, ALU.subtract)
            nc.vector.tensor_scalar(part_mask[:, 1:2], ident[0:3, 2:3], -1.0, None, ALU.mult).then_inc(parts, 1)
            dve.wait_ge(bias_loaded, 16)
            nc.vector.tensor_scalar(bias3[:, 0:2, :], bias3[:, 0:2, :], 1.0, None, ALU.add).then_inc(parts, 1)

            def split_rows(first, last, done):
                rows = slice(first, last)
                source = bias3
                for i in range(2):
                    dve.wait_ge(parts, done + 2 * i)
                    nc.vector.tensor_copy(high[i][:, rows, :], source[:, rows, :]).then_inc(parts, 1)
                    dve.wait_ge(parts, done + 2 * i + 1)
                    dest = bias_parts if i else rest
                    nc.vector.scalar_tensor_tensor(dest[:, rows, :], high[i][:, rows, :], part_mask[:, i:i + 1],
                                                   source[:, rows, :], ALU.mult, ALU.add).then_inc(parts, 1)
                    source = rest

            split_rows(0, 2, 2)
            normalise("n1", n1[0], x_chunk(0, 0), 1, n1_ok)
            dve.wait_ge(cols_mm, 1)
            raw_cols = banks[1][:, 0:4 * S].rearrange("p (k s) -> p k s", k=4)
            nc.vector.tensor_scalar(modT[:, CA:CB + 1, :], raw_cols[:, CA:CB + 1, :], 1.0, None, ALU.add)
            nc.vector.tensor_copy(modT[:, SA:SB + 1, :], raw_cols[:, SA:SB + 1, :]).then_inc(cols_ok, 1)
            dve.wait_ge(row_loaded, 16)
            gate_rows()
            dve.wait_ge(bv_mm, 1)
            nc.vector.tensor_tensor(bv_rows[:, :], banks[3][0:S, 0:D], row_in[:, 2, :], ALU.add).then_inc(bv_ok, 1)

            def shift_columns():
                for i in range(2):
                    mu = cols[:, S + 2 + i:S + 3 + i]
                    nc.vector.tensor_scalar(modT[:, FIRST + i, :], modT[:, SB, :], mu, None, ALU.mult)
                    last = nc.vector.tensor_scalar(modT[:, MOVE + i, :], modT[:, CB, :], mu, None, ALU.mult)
                last.then_inc(shift_cols, 1)
                dve.wait_ge(shift_cols, 1)
                nc.vector.tensor_tensor(modT[:, KEEP:KEEP + 2, :], modT[:, CB:CB + 1, :].broadcast_to([128, 2, S]),
                                        modT[:, MOVE:MOVE + 2, :], ALU.subtract).then_inc(shift_cols, 1)

            def step_end(j, off):
                t = 2 * j + off
                sd, sc = t - 2, t - 4
                z = chunked(banks[6])
                if live(j, off - 2):
                    need(dve, z_mm, sd + 1)
                    norm_stats("z", lambda c: z[:, c, :])
                if live(j, off - 4):
                    need(dve, tanh_ok, sc + 1)
                    need(dve, v_mm, sc + 1)
                    nc.vector.scalar_tensor_tensor(prod[:, :, :], tanh_r[:, :, :], 1.0, chunked(banks[5]), ALU.add,
                                                   ALU.mult).then_inc(prod_ok, 1)
                if live(j, off - 2):
                    norm_mv("z", sd + 1)

            def step(j, off):
                t = 2 * j + off
                sa, sb_, sd, sp_, sc = t, t - 1, t - 2, t - 3, t - 4
                u = banks[1][:, 0:NC * (D + H)].rearrange("p (c e) -> p c e", c=NC)
                y = chunked(banks[1])
                z = chunked(banks[6])
                x2_p = x2[(off - 3) % 2]
                step_end(j, off - 1)
                def q_elu():
                    need(dve, expq_ok, sa + 1)
                    nc.vector.scalar_tensor_tensor(qT[:, :], exp_q[:, :], 1.0, banks[5][:, 0:L], ALU.min,
                                                   ALU.max).then_inc(q_ok, 1)

                def mix():
                    need(dve, keep_ok, sc + 1)
                    for i in range(2):
                        last = nc.vector.scalar_tensor_tensor(mixT[:, i, :], banks[2][:, 0:L], modT[:, MOVE + i, bass.ds(sc, 1)],
                                                              keepT[:, i, :], ALU.mult, ALU.add)
                    last.then_inc(mix_ok, 1)

                def next_n1():
                    need(dve, aks_mm, sa)
                    normalise("n1", n1[(off + 1) % 2], x_chunk(j, off + 1), sa + 2, n1_ok)

                if live(j, off + 1):
                    if isinstance(j, int) and t in (0, 3):
                        dve.wait_ge(x_in[1 if t == 0 else 2], 16)
                    norm_stats("n1", x_chunk(j, off + 1))
                    need(dve, stats_ok["n1"], sa + 2)
                if live(j, off - 1):
                    need(dve, u_mm, sb_ + 1)
                    nc.vector.tensor_scalar(den[:, :, :], u[:, :, D:D + H], EPS_ATTN, None, ALU.add).then_inc(den_ok, 1)
                if live(j, off + 1):
                    norm_mv("n1")
                if live(j, off - 1):
                    need(dve, den_ok, sb_ + 1)
                    nc.vector.reciprocal(rden[:, :, :], den[:, :, :]).then_inc(rden_ok, 1)
                if draining(j, off):
                    mix()
                if live(j, off - 3):
                    need(dve, rstd_ok["z"], sp_ + 1)
                    for c in range(NC):
                        last = nc.vector.scalar_tensor_tensor(z1[:, c, :], z[:, c, :], mv["z"][:, c, 0:1],
                                                              gm_rows[(off - 3) % 2][:, G_ROW, :], ALU.subtract, ALU.mult)
                    last.then_inc(z1_ok, 1)
                if live(j, off - 1):
                    need(dve, rden_ok, sb_ + 1)
                    for c in range(NC):
                        last = nc.vector.tensor_tensor(att[:, c, :].rearrange("p (h d) -> p h d", h=H),
                                                       u[:, c, 0:D].rearrange("p (h d) -> p h d", h=H),
                                                       rden[:, c, :].unsqueeze(2).broadcast_to([128, H, DH]), ALU.mult)
                    last.then_inc(att_ok, 1)
                if live(j, off):
                    need(dve, expk_ok, sa + 1)
                    nc.vector.scalar_tensor_tensor(k_sb[:, :, :], exp_k[:, :, :], 1.0, chunked(banks[4]), ALU.min,
                                                   ALU.max).then_inc(k_ok, 1)
                if live(j, off - 3):
                    need(dve, xb_ok, sp_ + 1)
                    need(dve, out_ok, sp_ - 1)
                    need(dve, z1_ok, sp_ + 1)
                    for c in range(NC):
                        last = nc.vector.scalar_tensor_tensor(x2_p[:, c, :], z1[:, c, :], rstd["z"][:, c:c + 1],
                                                              xb[:, c, :], ALU.mult, ALU.add)
                    last.then_inc(x2_ok, 1)
                    need(dve, x2_ok, sp_ + 1)
                    norm_stats("n3", lambda c: x2_p[:, c, :])
                if live(j, off - 4) and not draining(j, off):
                    mix()
                if live(j, off - 3):
                    norm_mv("n3", sp_ + 1)
                if isinstance(j, int) and t < 3:
                    q_elu()
                if live(j, off + 1):
                    next_n1()
                if live(j, off - 1):
                    need(dve, y_mm, sb_ + 1)
                    norm_stats("ny", lambda c: y[:, c, :])
                if live(j, off) and not (isinstance(j, int) and t < 3):
                    q_elu()
                if live(j, off - 1):
                    norm_mv("ny", sb_ + 1)
                if live(j, off - 3):
                    need(dve, h2T_mm, sp_)
                    normalise("n3", n3, lambda c: x2_p[:, c, :], sp_ + 1, n3_ok)
                if live(j, off):
                    need(dve, a_ok, sa + 1)
                    need(dve, bv_in[off % 2], 16 * (j + off // 2 + 1), 16 * S)
                    need(dve, kv_mm, sa + 1)
                    nc.vector.scalar_tensor_tensor(kv_raw[:, :], bv_row[off % 2][:, :], ksum, banks[3][:, 0:D],
                                                   ALU.mult, ALU.add).then_inc(kvr_ok, 1)
                if live(j, off - 1):
                    normalise("ny", ny, lambda c: y[:, c, :], sb_ + 1, ny_ok)
                if isinstance(j, int) and t == 0:
                    split_rows(2, 4, 6)
                    shift_columns()

            steps(dve, step)
            step_end(0, S + STEPS_DEEP - 1)

        @block.tensor
        def _(pe):
            pe.wait_ge(const_pool, 3)
            for _ in range(WARM):
                nc.tensor.matmul(banks[6][:, 0:128], ident[:, :], ident[:, :], start=True, stop=True)
            pe.wait_ge(silu_ok, 2)
            pe.wait_ge(wmod_loaded, 16)
            for i, chunk in enumerate((1, 4, 0, 3)):
                last = nc.tensor.matmul(banks[1][:, i * S:(i + 1) * S], wmod[:, chunk * D:(chunk + 1) * D], siluT[:, :],
                                        start=True, stop=True)
            last.then_inc(cols_mm, 1)
            for i, chunk in enumerate((2, 5)):
                last = nc.tensor.matmul(banks[2][0:S, i * D:(i + 1) * D], siluT[:, :], wmod[:, chunk * D:(chunk + 1) * D],
                                        start=True, stop=True)
            last.then_inc(gates_mm, 1)

            def bv_product():
                pe.wait_ge(cols_ok, 1)
                pe.wait_ge(wvo_loaded, 16)
                nc.tensor.matmul(banks[3][0:S, 0:D], modT[:, SA, :], wv, start=True, stop=True).then_inc(bv_mm, 1)

            def transpose_in(bank, tile, signal):
                for c in range(NC):
                    last = nc.tensor.transpose(bank[:, c * 128:(c + 1) * 128], tile[:, c, :], ident[:, :])
                last.then_inc(signal, 1)

            def bias_into(bank, i):
                nc.tensor.matmul(chunked(bank), ones3[:, 0:128], bias_parts[:, i:i + 1, :].broadcast_to([3, NC, D]),
                                 start=True, stop=False)

            def residual_into(bank, tileT, c):
                return nc.tensor.matmul(bank[:, c * D:(c + 1) * D], tileT[:, c * 128:(c + 1) * 128], ident[:, :],
                                        start=False, stop=False, is_transpose=True)

            def feed_forward_out(f0, f1):
                for f in range(f0, f1):
                    for c in range(NC):
                        last = nc.tensor.matmul(banks[6][:, c * D:(c + 1) * D], hid[:, f, c * 128:(c + 1) * 128], w2[:, f, :],
                                                start=False, stop=(f == FF - 1 and c == NC - 1))
                return last

            def mix_products(j, off):
                sc = 2 * j + off - 4
                if live(j, off - 4):
                    if isinstance(j, int) and sc == 0:
                        pe.wait_ge(mix_loaded, 16)
                    need(pe, mix_ok, sc + 1)
                    nc.tensor.matmul(banks[2][:, 0:L], wkT, mixT[:, 1, :], start=True, stop=True).then_inc(kk_mm, 1)
                    need(pe, k_ok, sc + 5)
                    for c in range(NC):
                        last = nc.tensor.matmul(banks[4][:, c * D:(c + 1) * D], mixT[:, 0, c * 128:(c + 1) * 128], wrT,
                                                start=True, stop=True)
                    last.then_inc(r_mm, 1)

            def step(j, off):
                t = 2 * j + off
                sa, sb_, sd, sc = t, t - 1, t - 2, t - 4
                if live(j, off):
                    need(pe, n1_ok, sa + 1)
                    need(pe, attT_ok, sa - 1)
                    transpose_in(banks[0], n1[off % 2], hT_mm)
                    if isinstance(j, int) and t == 0:
                        bv_product()
                        pe.wait_ge(kq_loaded, 16)
                        pe.wait_ge(parts, 6)
                if live(j, off - 2):
                    need(pe, ny_ok, sd + 1)
                    need(pe, hida_ok, sd)
                    transpose_in(banks[7], ny, x1T_mm)
                if live(j, off - 4):
                    need(pe, n3_ok, sc + 1)
                    need(pe, reluk_ok, sc)
                    transpose_in(banks[2], n3, h2T_mm)
                if live(j, off - 1):
                    need(pe, s16_ok, sb_ + 1)
                    need(pe, kv_ok, sb_ + 1)
                    need(pe, q_ok, sb_ + 1)
                    need(pe, ny_ok, sb_)
                    for c in range(NC):
                        last = nc.tensor.matmul(banks[1][:, c * (D + H):(c + 1) * (D + H)], qT[:, c * 128:(c + 1) * 128],
                                                kvs[:, :], start=True, stop=True)
                    last.then_inc(u_mm, 1)
                if live(j, off):
                    need(pe, hT_ok, sa + 1)
                    need(pe, k_ok, sa)
                    need(pe, tanh_ok, sa - 4)
                    bias_into(banks[4], 0)
                    for c in range(NC):
                        last = nc.tensor.matmul(banks[4][:, c * D:(c + 1) * D], hT[off % 2][:, c * 128:(c + 1) * 128],
                                                wk, start=False, stop=(c == NC - 1))
                    last.then_inc(k_mm, 1)
                    need(pe, q_ok, sa)
                    need(pe, prod_ok, sa - 4)
                    nc.tensor.matmul(banks[5][:, 0:L], bias_parts[:, 1, :], ones3[:, :], start=True, stop=False)
                    nc.tensor.matmul(banks[5][:, 0:L], wq, hT[off % 2][:, :], start=False, stop=True).then_inc(q_mm, 1)
                if live(j, off - 2):
                    if isinstance(j, int) and sd == 0:
                        pe.wait_ge(w12_loaded, 16)
                    need(pe, x1T_ok, sd + 1)
                    for f in range(2):
                        last = nc.tensor.matmul(banks[7][:, f * L:(f + 1) * L], w1[:, f * 128:(f + 1) * 128], x1T[:, :],
                                                start=True, stop=True)
                    last.then_inc(w1a_mm, 1)
                    if draining(j, off):
                        need(pe, kvr_ok, S)
                        need(pe, hidb_ok, sd)
                    else:
                        need(pe, z1_ok, sd)
                    for f in range(2):
                        last = nc.tensor.matmul(hidden_bank(j, off)[:, f * L:(f + 1) * L], w1[:, (2 + f) * 128:(3 + f) * 128],
                                                x1T[:, :], start=True, stop=True)
                    last.then_inc(w1b_mm, 1)
                if draining(j, off):
                    mix_products(j, off)
                if live(j, off - 1):
                    need(pe, att_ok, sb_ + 1)
                    need(pe, hT_ok, sb_ + 2)
                    transpose_in(banks[0], att, attT_mm)
                if live(j, off):
                    need(pe, k_ok, sa + 1)
                    need(pe, kvr_ok, sa)
                    for c in range(NC):
                        nc.tensor.matmul(banks[3][:, 0:D], n1[off % 2][:, c, :], k_sb[:, c, :], start=(c == 0),
                                         stop=(c == NC - 1))
                    for c in range(NC):
                        last = nc.tensor.matmul(banks[3][:, D:D + 1], k_sb[:, c, :], ones[:, :], start=(c == 0),
                                                stop=(c == NC - 1))
                    last.then_inc(aks_mm, 1)
                if live(j, off - 1):
                    if isinstance(j, int) and sb_ == 0:
                        pe.wait_ge(parts, 10)
                    need(pe, attT_ok, sb_ + 1)
                    bias_into(banks[1], 2)
                    for c in range(NC):
                        residual_into(banks[1], hT[(off - 1) % 2], c)
                        last = nc.tensor.matmul(banks[1][:, c * D:(c + 1) * D], attT[:, c * 128:(c + 1) * 128], wo,
                                                start=False, stop=(c == NC - 1))
                    last.then_inc(y_mm, 1)
                if not draining(j, off):
                    mix_products(j, off)
                if live(j, off - 2):
                    need(pe, hidb_ok, sd + 1)
                    if draining(j, off):
                        need(pe, z1_ok, sd)
                    bias_into(banks[6], 3)
                    for c in range(NC):
                        residual_into(banks[6], x1T, c)
                if live(j, off):
                    need(pe, a_ok, sa + 1)
                    need(pe, wvm_ok, sa + 1)
                    nc.tensor.matmul(banks[3][:, 0:D], a_sb[:, 0:D], wv_mod[:, :], start=True, stop=True).then_inc(kv_mm, 1)
                if live(j, off - 2):
                    feed_forward_out(0, 2)
                if live(j, off - 4):
                    need(pe, ksq_ok, sc + 1)
                    need(pe, wvg_ok, sc + 1)
                    need(pe, q_ok, sc + 5)
                    for c in range(NC):
                        last = nc.tensor.matmul(banks[5][:, c * D:(c + 1) * D], ksqT[:, c * 128:(c + 1) * 128], wv_gate[:, :],
                                                start=True, stop=True)
                    last.then_inc(v_mm, 1)
                if live(j, off - 2):
                    feed_forward_out(2, FF).then_inc(z_mm, 1)

            steps(pe, step)


def kernel(**inputs):
    import concourse.bacc as bacc
    from concourse.bass_utils import run_bass_kernel_spmd

    nc = bacc.Bacc("TRN2", target_bir_lowering=False, num_devices=1)
    attn = {n: inputs[f"L0_attn_{n}"] for n in ("x", "Wq", "bq", "Wk", "bk", "Wv", "bv", "Wo", "bo", "W1", "b1", "W2", "b2",
                                               "g1", "beta1", "g2", "beta2")}
    ffn = {n: inputs[f"L0_ffn_{n}"] for n in ("W_r", "W_k", "W_v", "mu_r", "mu_k")}
    laid_out = {
        "x": attn["x"],
        "wmod": inputs["L0_wmod"],
        "cols": np.concatenate([np.asarray(inputs["L0_c"]).T]
                               + [np.reshape(v, (-1, 128)).T for v in (attn["g1"], attn["beta1"], ffn["mu_r"],
                                                                      ffn["mu_k"], attn["b1"])], axis=1),
        "kqvo": np.stack([attn[n] for n in ("Wk", "Wq", "Wv", "Wo")], axis=1),
        "w12": np.stack([attn["W1"], np.reshape(attn["W2"], (FF, 128, D)).transpose(1, 0, 2).reshape(128, FF * D)], axis=1),
        "mix_w": np.stack([np.asarray(ffn[n]).T for n in ("W_r", "W_k", "W_v")], axis=1),
        "bias": np.stack([attn[n] for n in ("bk", "bq", "bo", "b2")]),
        "rows": np.stack([attn[n] for n in ("g2", "beta2", "bv")]),
    }
    arrays, aps = {}, {}
    for name, arr in laid_out.items():
        arr = np.ascontiguousarray(arr)
        arrays[f"in_{name}"] = arr
        aps[name] = nc.dram_tensor(f"in_{name}", arr.shape, mybir.dt.from_np(arr.dtype), kind="ExternalInput").ap()
    out = nc.dram_tensor("out", (S, L, D), F32, kind="ExternalOutput").ap()
    scratch = {"bv": nc.dram_tensor("bv_rows_dram", (S, D), F32, kind="Internal").ap(),
               "rows": nc.dram_tensor("mod_rows_dram", (S, 3, D), F32, kind="Internal").ap()}
    build(nc, aps, out, scratch)
    r = run_bass_kernel_spmd(nc, [arrays], core_ids=[0])
    return r.results[0]["out"]
```

```python
from contextlib import ExitStack

import numpy as np

import concourse.bass as bass
from concourse import mybir

F32 = mybir.dt.float32
BF16 = mybir.dt.bfloat16
ALU = mybir.AluOpType
ACT = mybir.ActivationFunctionType

S, L, D = 16, 256, 128
NC = L // 128
H, DH = 16, 8
FF = 4
EPS_ATTN = 1e-6
EPS_LN = 1e-5
WARM = 8
STEPS_DEEP = 4
G1, BETA1, MU, B1, BQ, B2, G2, BETA2, BO, COLS = (S + i for i in (0, 1, 2, 4, 8, 9, 10, 11, 12, 15))
CA, CB, SA, SB, MOVE, KEEP, FIRST, SABO, KINDS = 0, 1, 2, 3, 4, 6, 8, 10, 11
G_ROW, GB_ROW, GATE_ROW = range(3)


def build(nc, a, out, scratch):
    with ExitStack() as ctx:
        def sb(name, shape, dt=F32):
            return ctx.enter_context(nc.sbuf_tensor(name, shape, dt))

        def sem(name):
            return ctx.enter_context(nc.semaphore(name))

        banks = [ctx.enter_context(nc.psum_tensor(f"bank{i}", [128, 512], F32)) for i in range(8)]

        kqvo = sb("kqvo", [128, 4, D])
        wk, wq, wv, wo = (kqvo[:, i, :] for i in range(4))
        w12 = sb("w12", [128, 2, FF * 128])
        w1, w2 = w12[:, 0, :], w12[:, 1, :].rearrange("p (f d) -> p f d", f=FF)
        mix_w = sb("mix_w", [128, 3, D])
        wrT, wkT, wvT = (mix_w[:, i, :] for i in range(3))
        cols = sb("cols", [128, COLS])
        wmod = sb("wmod", [128, 6 * D])
        ident = sb("ident", [128, 128])
        ones = sb("ones", [128, 1])
        headmask = sb("headmask", [128, H, DH])
        power = sb("power", [128, NC])
        eps = sb("eps", [128, NC])
        ones3 = sb("ones3", [3, 128], BF16)
        bq_col = sb("bq_col", [128, 1])
        b1_cols = sb("b1_cols", [128, FF])
        beta1_b2 = sb("beta1_b2", [128, 1])
        neg1 = sb("neg1", [128, 1])
        table_load = sb("table_load", [128, 1])
        tanh_c = sb("tanh_c", [128, S])
        silu2 = sb("silu2", [128, S])
        siluT = sb("siluT", [128, S])
        modT = sb("modT", [128, KINDS, S])
        bv_in_rows = sb("bv_in_rows", [S, D])
        gate_sign, gate_pos, gate_size, gates = (sb(n, [128, 2, S]) for n in ("gate_sign", "gate_pos", "gate_size", "gates"))
        gate_cols = sb("gate_cols", [128, 3, S])
        warm = sb("warm", [128, 128])
        mod_rows = sb("mod_rows", [S, 3, D])
        bv_rows = sb("bv_rows", [S, D])
        bias3 = sb("bias3", [3, D])
        bias_k = sb("bias_k", [3, D])
        part_mask = sb("part_mask", [3, 2])
        high = [sb(f"high{i}", [3, D], BF16) for i in range(2)]
        rest = sb("rest", [3, D])
        bias_parts = sb("bias_parts", [3, D], BF16)
        x_all = sb("x_all", [128, S * NC, D])
        bv_row = [sb(f"bv_row{p}", [128, D]) for p in range(2)]
        gm_rows = [sb(f"gm_rows{p}", [128, 3, D]) for p in range(2)]
        n1 = [sb(f"n1_{p}", [128, NC, D]) for p in range(2)]
        hT = [sb(f"hT{p}", [128, L]) for p in range(2)]
        exp_k = sb("exp_k", [128, NC, D])
        k_sb = sb("k_sb", [128, NC, D])
        k_pair = sb("k_pair", [128, D])
        exp_q = sb("exp_q", [128, L])
        relu_q = sb("relu_q", [128, L])
        qT = sb("qT", [128, L])
        a_sb = sb("a_sb", [128, D + 1])
        wv_mod = sb("wv_mod", [128, D])
        ksum = a_sb[:, D:D + 1]
        kv_raw = sb("kv_raw", [128, D])
        kvs = sb("kvs", [128, D + H])
        den = sb("den", [128, NC, H])
        rden = sb("rden", [128, NC, H])
        att = sb("att", [128, NC, D])
        attT = sb("attT", [128, L])
        ny = sb("ny", [128, NC, D])
        x1T = sb("x1T", [128, L])
        hid = sb("hid", [128, FF, L])
        z1 = sb("z1", [128, NC, D])
        xb = sb("xb", [128, NC, D])
        x2 = [sb(f"x2_{p}", [128, NC, D]) for p in range(2)]
        n3 = sb("n3", [128, NC, D])
        keepT = sb("keepT", [128, 2, L])
        mixT = sb("mixT", [128, 2, L])
        tanh_r = sb("tanh_r", [128, NC, D])
        relu_k = sb("relu_k", [128, L])
        ksqT = sb("ksqT", [128, L])
        wv_gate = sb("wv_gate", [128, D])
        prod = sb("prod", [128, NC, D])
        out_sb = sb("out_sb", [128, NC, D])
        NORMS = ("n1", "ny", "z", "n3")
        stats = {n: sb(f"stats_{n}", [128, NC, 6]) for n in NORMS}
        mv = {n: sb(f"mv_{n}", [128, NC, 2]) for n in NORMS}
        vare = {n: sb(f"vare_{n}", [128, NC]) for n in NORMS}
        rstd = {n: sb(f"rstd_{n}", [128, NC]) for n in NORMS}

        x_in = [sem(f"x_in{i}") for i in range(3)]
        cols_loaded, kq_loaded = sem("cols_loaded"), sem("kq_loaded")
        wmod_loaded = [sem(f"wmod_loaded{i}") for i in range(2)]
        wvo_loaded, w12_loaded, mix_loaded = map(sem, ("wvo_loaded", "w12_loaded", "mix_loaded"))
        bv_loaded, bias_loaded, bv_stored, rows_stored = map(sem, ("bv_loaded", "bias_loaded", "bv_stored", "rows_stored"))
        bv_in = [sem(f"bv_in{p}") for p in range(2)]
        gm_in = [sem(f"gm_in{p}") for p in range(2)]
        stored = sem("stored")
        const_pool, const_dve = sem("const_pool"), sem("const_dve")
        tanh_c_ok, silu_ok = sem("tanh_c_ok"), sem("silu_ok")
        warm_ok, gates_turned, rows_ok = sem("warm_ok"), sem("gates_turned"), sem("rows_ok")
        cols_mm, bv_mm, bias_mm, b1_mm = map(sem, ("cols_mm", "bv_mm", "bias_mm", "b1_mm"))
        bq_ok, b1_ok = sem("bq_ok"), sem("b1_ok")
        parts, cols_ok, bv_ok = sem("parts"), sem("cols_ok"), sem("bv_ok")
        gate_ok, shift_cols = sem("gate_ok"), sem("shift_cols")
        (hT_mm, u_mm, x1T_mm, v_mm, k_mm, q_mm, attT_mm, w1a_mm, w1b_mm, h2T_mm, y_mm, aks_mm, z_mm, r_mm,
         kk_mm, kv_mm) = map(sem, ("hT_mm u_mm x1T_mm v_mm k_mm q_mm attT_mm w1a_mm w1b_mm h2T_mm y_mm aks_mm "
                                   "z_mm r_mm kk_mm kv_mm").split())
        (hT_ok, x1T_ok, expk_ok, expq_ok, attT_ok, hida_ok, hidb_ok, keep_ok, a_ok, tanh_ok, reluk_ok, ksq_ok) = map(
            sem, ("hT_ok x1T_ok expk_ok expq_ok attT_ok hida_ok hidb_ok keep_ok a_ok tanh_ok reluk_ok "
                 "ksq_ok").split())
        (n1_ok, ny_ok, n3_ok, k_ok, q_ok, wvm_ok, kvr_ok, den_ok, rden_ok, att_ok, z1_ok, x2_ok, mix_ok,
         prod_ok) = map(sem, ("n1_ok ny_ok n3_ok k_ok q_ok wvm_ok kvr_ok den_ok rden_ok att_ok z1_ok x2_ok mix_ok "
                              "prod_ok").split())
        stats_ok = {n: sem(f"stats_ok_{n}") for n in NORMS}
        mv_ok = {n: sem(f"mv_ok_{n}") for n in NORMS}
        mixk_ok, last_ok = sem("mixk_ok"), sem("last_ok")
        s16_ok, kv_ok, xb_ok, wvg_ok, out_ok, pair_ok = map(sem, "s16_ok kv_ok xb_ok wvg_ok out_ok pair_ok".split())
        vare_ok = {n: sem(f"vare_ok_{n}") for n in NORMS}
        rstd_ok = {n: sem(f"rstd_ok_{n}") for n in NORMS}

        x_dram = a["x"].rearrange("s (c p) d -> p (s c) d", p=128)
        out_dram = out.rearrange("s (c p) d -> s p c d", p=128)

        def chunked(bank):
            return bank[:, 0:NC * D].rearrange("p (c d) -> p c d", c=NC)

        def steps(eng, step):
            for t in range(STEPS_DEEP + 1):
                step(0, t)
            with eng.Fori(STEPS_DEEP // 2, S // 2 - 1) as j:
                for off in (1, 2):
                    step(j, off)
            for t in range(S - 1, S + STEPS_DEEP):
                step(0, t)

        def live(j, off):
            return not isinstance(j, int) or 0 <= off < S

        def draining(j, off):
            return isinstance(j, int) and off >= S

        def hidden_bank(j, off):
            return banks[3] if draining(j, off) else banks[6]

        def need(eng, signal, count, most=S):
            if isinstance(count, int):
                count = min(count, most)
                if count <= 0:
                    return
            eng.wait_ge(signal, count)

        block = ctx.enter_context(nc.Block())

        @block.sync
        def _(sp):
            sp.dma_start(x_all[:, 0:NC, :], x_dram[:, 0:NC, :]).then_inc(x_in[0], 16)
            sp.dma_start(wmod[:, 0:2 * D], a["wmod"][:, 0:2 * D]).then_inc(wmod_loaded[0], 16)
            sp.dma_start(kqvo[:, 0:2, :], a["kqvo"][:, 0:2, :]).then_inc(kq_loaded, 16)
            sp.dma_start(kqvo[:, 2:4, :], a["kqvo"][:, 2:4, :]).then_inc(wvo_loaded, 16)
            sp.dma_start(x_all[:, NC:4 * NC, :], x_dram[:, NC:4 * NC, :]).then_inc(x_in[1], 16)
            sp.dma_start(wmod[:, 2 * D:], a["wmod"][:, 2 * D:]).then_inc(wmod_loaded[1], 16)
            sp.wait_ge(bv_ok, 1)
            sp.dma_start(scratch["bv"], bv_rows[:, :]).then_inc(bv_stored, 16)
            sp.wait_ge(bv_stored, 16)

            def load_bv(j, off):
                if not live(j, off):
                    return
                s, p = 2 * j + off, off % 2
                need(sp, kvr_ok, s - 1)
                sp.dma_start(bv_row[p][:, :], scratch["bv"][bass.ds(s, 1), :].broadcast_to([128, D])).then_inc(bv_in[p], 16)

            def load_gm(j, off):
                if not live(j, off):
                    return
                s, p = 2 * j + off, off % 2
                need(sp, wvg_ok, s - 1)
                sp.dma_start(gm_rows[p][:, :, :],
                             scratch["rows"][bass.ds(s, 1), :, :].broadcast_to([128, 3, D])).then_inc(gm_in[p], 16)

            def store(j, off):
                if not live(j, off):
                    return
                s = 2 * j + off
                need(sp, out_ok, s + 1)
                if isinstance(j, int) and s == S - 1:
                    sp.dma_start(out_dram[s, :, 0, :], out_sb[:, 0, :]).then_inc(stored, 16)
                else:
                    sp.dma_start(out_dram[bass.ds(s, 1), :, :, :].squeeze(0), out_sb[:, :, :]).then_inc(stored, 16)

            load_bv(0, 0)
            load_bv(0, 1)
            sp.dma_start(w12[:, :, :], a["w12"]).then_inc(w12_loaded, 16)
            sp.dma_start(x_all[:, 4 * NC:, :], x_dram[:, 4 * NC:, :]).then_inc(x_in[2], 16)
            sp.wait_ge(rows_ok, 1)
            sp.dma_start(scratch["rows"], mod_rows[:, :, :]).then_inc(rows_stored, 16)
            sp.wait_ge(rows_stored, 16)

            def step(j, off):
                if not isinstance(j, int) or off > 0:
                    load_bv(j, off + 1)
                load_gm(j, off - 2)
                store(j, off - 4)

            steps(sp, step)
            sp.wait_ge(stored, 16 * (S + 1))

        @block.scalar
        def _(act):
            act.dma_start(cols[:, :], a["cols"]).then_inc(cols_loaded, 16)
            act.wait_ge(const_dve, 2)
            nc.scalar.activation(table_load[:, :], neg1[:, :], ACT.Tanh)
            act.dma_start(bias3[:, :], a["bk"].rearrange("(a d) -> a d", a=1).broadcast_to([3, D])).then_inc(bias_loaded, 16)
            act.wait_ge(cols_loaded, 16)
            nc.scalar.activation(tanh_c[:, :], cols[:, 0:S], ACT.Tanh, scale=0.5).then_inc(tanh_c_ok, 1)
            act.dma_start(mix_w[:, :, :], a["mix_w"]).then_inc(mix_loaded, 16)

            act.wait_ge(cols_ok, 1)

            def mod_col(kind, s):
                return modT[:, kind, bass.ds(s, 1)]

            def step(j, off):
                t = 2 * j + off
                sa, sb_, sd, sc = t, t - 1, t - 2, t - 4
                if live(j, off):
                    need(act, y_mm, sa - 1)
                    need(act, hT_mm, sa + 1)
                    nc.scalar.activation(hT[off % 2][:, :], banks[0][:, 0:L], ACT.Identity, scale=mod_col(CA, sa),
                                         bias=mod_col(SABO, sa)).then_inc(hT_ok, 1)
                if live(j, off - 2):
                    need(act, x1T_mm, sd + 1)
                    nc.scalar.activation(x1T[:, :], banks[7][:, 0:L], ACT.Identity, scale=cols[:, G1:G1 + 1],
                                         bias=beta1_b2[:, :]).then_inc(x1T_ok, 1)
                if live(j, off - 4):
                    need(act, mix_ok, sc)
                    need(act, h2T_mm, sc + 1)
                    if isinstance(j, int) and sc == 0:
                        act.wait_ge(shift_cols, 2)
                    nc.scalar.activation(keepT[:, :, 0:1], modT[:, FIRST:FIRST + 2, bass.ds(sc, 1)], ACT.Copy)
                    for i in range(2):
                        last = nc.scalar.activation(keepT[:, i, 1:L], banks[2][:, 0:L - 1], ACT.Identity,
                                                    scale=mod_col(KEEP + i, sc), bias=mod_col(SB, sc))
                    last.then_inc(keep_ok, 1)
                if live(j, off):
                    need(act, k_mm, sa + 1)
                    nc.scalar.activation(exp_k[:, :, :], chunked(banks[4]), ACT.Exp, bias=neg1[:, :]).then_inc(expk_ok, 1)
                    if isinstance(j, int) and t == 0:
                        act.wait_ge(bq_ok, 1)
                    need(act, q_ok, sa)
                    need(act, q_mm, sa + 1)
                    nc.scalar.activation(exp_q[:, :], banks[5][:, 0:L], ACT.Exp, bias=bq_col[:, :])
                    nc.scalar.activation(relu_q[:, :], banks[5][:, 0:L], ACT.Relu, bias=bq_col[:, :]).then_inc(expq_ok, 1)
                if live(j, off - 2):
                    if isinstance(j, int) and sd == 0:
                        act.wait_ge(b1_ok, 1)
                    need(act, w1a_mm, sd + 1)
                    nc.scalar.activation(hid[:, 0, :], banks[7][:, 0:L], ACT.Relu, bias=b1_cols[:, 0:1])
                if live(j, off - 1):
                    need(act, attT_mm, sb_ + 1)
                    nc.scalar.activation(attT[:, :], banks[0][:, 0:L], ACT.Copy).then_inc(attT_ok, 1)
                if live(j, off - 2):
                    nc.scalar.activation(hid[:, 1, :], banks[7][:, L:2 * L], ACT.Relu, bias=b1_cols[:, 1:2]).then_inc(hida_ok, 1)
                if live(j, off - 2):
                    need(act, w1b_mm, sd + 1)
                    for f in range(2, FF):
                        last = nc.scalar.activation(hid[:, f, :], hidden_bank(j, off)[:, (f - 2) * L:(f - 1) * L], ACT.Relu,
                                                    bias=b1_cols[:, f:f + 1])
                    last.then_inc(hidb_ok, 1)
                if live(j, off):
                    act.wait_ge(wvo_loaded, 16)
                    need(act, kv_mm, sa)
                    nc.scalar.activation(wv_mod[:, :], wv, ACT.Copy, scale=mod_col(CA, sa)).then_inc(wvm_ok, 1)
                    need(act, aks_mm, sa + 1)
                    nc.scalar.activation(a_sb[:, :], banks[3][:, 0:D + 1], ACT.Copy).then_inc(a_ok, 1)
                if live(j, off - 4):
                    need(act, kk_mm, sc + 1)
                    nc.scalar.activation(relu_k[:, :], banks[0][:, 0:L], ACT.Relu).then_inc(reluk_ok, 1)
                    need(act, reluk_ok, sc + 1)
                    nc.scalar.activation(ksqT[:, :], relu_k[:, :], ACT.Square).then_inc(ksq_ok, 1)
                    need(act, prod_ok, sc)
                    need(act, r_mm, sc + 1)
                    nc.scalar.activation(tanh_r[:, :, :], chunked(banks[4]), ACT.Tanh, scale=0.5).then_inc(tanh_ok, 1)
                if isinstance(j, int) and t == 1:
                    act.wait_ge(gates_turned, 1)
                    nc.scalar.activation(mod_rows[:, :, :], banks[2][0:S, D:4 * D].rearrange("p (k d) -> p k d", k=3),
                                         ACT.Copy).then_inc(rows_ok, 1)

            steps(act, step)
            act.wait_ge(last_ok, 2)
            act.dma_start(out_dram[S - 1, :, 1, :], out_sb[:, 1, :]).then_inc(stored, 16)

        @block.gpsimd
        def _(pool):
            nc.gpsimd.memset(ident[:, :], 0.0).then_inc(const_pool, 1)
            nc.gpsimd.memset(headmask[:, :, :], 1.0).then_inc(const_pool, 1)
            pool.wait_ge(const_pool, 2)
            nc.gpsimd.affine_select(out=ident[:, :], in_=ident[:, :], compare_op=ALU.not_equal, fill=1.0, base=0,
                                    pattern=[[-1, 128]], channel_multiplier=1).then_inc(const_pool, 1)
            nc.gpsimd.affine_select(out=headmask[:, :, :], in_=headmask[:, :, :], compare_op=ALU.is_ge, fill=0.0,
                                    base=0, pattern=[[-DH, H], [0, DH]], channel_multiplier=1).then_inc(const_pool, 1)
            pool.wait_ge(const_pool, 4)
            nc.gpsimd.affine_select(out=headmask[:, :, :], in_=headmask[:, :, :], compare_op=ALU.is_ge, fill=0.0,
                                    base=DH - 1, pattern=[[DH, H], [0, DH]], channel_multiplier=-1).then_inc(const_pool, 1)
            pool.dma_start(bv_in_rows[:, :], a["bv"].rearrange("(a d) -> a d", a=1).broadcast_to([S, D])).then_inc(bv_loaded, 16)
            pool.wait_ge(const_dve, 5)

            def norm_scale(name, count):
                need(pool, mv_ok[name], count)
                nc.gpsimd.tensor_tensor(vare[name][:, :], mv[name][:, :, 1], eps[:, :], ALU.add).then_inc(vare_ok[name], 1)
                need(pool, vare_ok[name], count)
                nc.gpsimd.tensor_tensor(rstd[name][:, :], vare[name][:, :], power[:, :], ALU.pow).then_inc(rstd_ok[name], 1)

            norm_scale("n1", 1)

            def step(j, off):
                t = 2 * j + off
                sa, sb_, sd, sp_, sc = t, t - 1, t - 2, t - 3, t - 4
                if live(j, off + 1):
                    norm_scale("n1", sa + 2)
                if live(j, off - 4):
                    need(pool, v_mm, sc)
                    if isinstance(j, int) and sc == 0:
                        pool.wait_ge(mix_loaded, 16)
                    nc.gpsimd.tensor_tensor(wv_gate[:, :], wvT, gm_rows[off % 2][:, GATE_ROW, :],
                                            ALU.mult).then_inc(wvg_ok, 1)
                if live(j, off):
                    need(pool, aks_mm, sa)
                    need(pool, k_ok, sa + 1)
                    nc.gpsimd.tensor_tensor(k_pair[:, :], k_sb[:, 0, :], k_sb[:, 1, :], ALU.add).then_inc(pair_ok, 1)
                y_first = isinstance(j, int) and t == S
                if y_first:
                    norm_scale("ny", sb_ + 1)
                if live(j, off - 3):
                    norm_scale("n3", sp_ + 1)
                if live(j, off):
                    need(pool, a_ok, sa + 1)
                    nc.gpsimd.tensor_tensor(kvs[:, D:D + H], headmask[:, :, 0], ksum.broadcast_to([128, H]),
                                            ALU.mult).then_inc(s16_ok, 1)
                if live(j, off - 1) and not y_first:
                    norm_scale("ny", sb_ + 1)
                if live(j, off):
                    need(pool, kvr_ok, sa + 1)
                    nc.gpsimd.tensor_tensor(kvs[:, 0:D], kv_raw[:, :], headmask[:, :, :].rearrange("p h d -> p (h d)"),
                                            ALU.mult).then_inc(kv_ok, 1)
                if live(j, off - 2):
                    need(pool, x2_ok, sd)
                    need(pool, gm_in[off % 2], 16 * (j + (off - 2) // 2 + 1), 16 * S)
                    nc.gpsimd.tensor_tensor(xb[:, :, :], x_all[:, bass.ds(NC * sd, NC), :],
                                            gm_rows[off % 2][:, GB_ROW:GB_ROW + 1, :].broadcast_to([128, NC, D]),
                                            ALU.add).then_inc(xb_ok, 1)
                    norm_scale("z", sd + 1)
                if live(j, off - 4):
                    need(pool, stored, 16 * sc, 16 * S)
                    need(pool, prod_ok, sc + 1)
                    part = slice(0, 1) if isinstance(j, int) and sc == S - 1 else slice(0, NC)
                    nc.gpsimd.tensor_tensor(out_sb[:, part, :], x2[off % 2][:, part, :], prod[:, part, :],
                                            ALU.add).then_inc(out_ok, 1)

            steps(pool, step)

        @block.vector
        def _(dve):
            nc.vector.memset(warm[:, :], 1.0).then_inc(warm_ok, 1)
            nc.vector.memset(ones[:, :], 1.0).then_inc(const_dve, 1)
            nc.vector.memset(neg1[:, :], -1.0).then_inc(const_dve, 1)
            nc.vector.memset(ones3[:, :], 1.0).then_inc(const_dve, 1)
            nc.vector.memset(eps[:, :], EPS_LN).then_inc(const_dve, 1)
            nc.vector.memset(power[:, :], -0.5).then_inc(const_dve, 1)

            def norm_stats(name, source):
                for c in range(NC):
                    ins = nc.vector.bn_stats(stats[name][:, c, :], source(c))
                ins.then_inc(stats_ok[name], 1)

            def norm_mv(name, count=None):
                if count is not None:
                    dve.wait_ge(const_dve, 1)
                    need(dve, stats_ok[name], count)
                for c in range(NC):
                    ins = nc.vector.bn_aggr(mv[name][:, c, :], stats[name][:, c, :])
                ins.then_inc(mv_ok[name], 1)

            def normalise(name, dest, source, count, signal):
                need(dve, rstd_ok[name], count)
                for c in range(NC):
                    last = nc.vector.tensor_scalar(dest[:, c, :], source(c), mv[name][:, c, 0:1], rstd[name][:, c:c + 1],
                                                   ALU.subtract, ALU.mult)
                last.then_inc(signal, 1)

            def gate_columns():
                raw = banks[2][:, 2 * S:4 * S].rearrange("p (k s) -> p k s", k=2)
                nc.vector.tensor_scalar(gate_sign[:, :, :], raw, 0.0, 2.0, ALU.is_ge, ALU.mult)
                nc.vector.tensor_scalar(gate_pos[:, :, :], raw, 0.25, None, ALU.max).then_inc(gate_ok, 1)
                dve.wait_ge(gate_ok, 1)
                nc.vector.scalar_tensor_tensor(gate_size[:, :, :], raw, -1.0, gate_pos[:, :, :], ALU.mult,
                                               ALU.max).then_inc(gate_ok, 1)
                dve.wait_ge(gate_ok, 2)
                nc.vector.scalar_tensor_tensor(gates[:, :, :], gate_sign[:, :, :], -1.0, gate_size[:, :, :], ALU.add,
                                               ALU.mult).then_inc(gate_ok, 1)
                dve.wait_ge(gate_ok, 3)
                nc.vector.tensor_scalar(gate_cols[:, G_ROW, :], gates[:, 0, :], cols[:, G2:G2 + 1], None, ALU.mult)
                nc.vector.tensor_scalar(gate_cols[:, GB_ROW, :], gates[:, 0, :], cols[:, BETA2:BETA2 + 1], None, ALU.mult)
                nc.vector.tensor_scalar(gate_cols[:, GATE_ROW, :], gates[:, 1, :], 0.5, None, ALU.mult).then_inc(gate_ok, 1)

            def x_chunk(j, off):
                return lambda c: x_all[:, bass.ds(NC * (2 * j + off) + c, 1), :].squeeze(1)

            dve.wait_ge(x_in[0], 16)
            norm_stats("n1", x_chunk(0, 0))
            norm_mv("n1", 1)
            dve.wait_ge(tanh_c_ok, 1)
            nc.vector.scalar_tensor_tensor(silu2[:, :], tanh_c[:, :], 1.0, cols[:, 0:S], ALU.add, ALU.mult).then_inc(silu_ok, 1)
            dve.wait_ge(silu_ok, 1)
            nc.vector.tensor_scalar(siluT[:, :], silu2[:, :], 0.5, None, ALU.mult).then_inc(silu_ok, 1)

            dve.wait_ge(const_pool, 3)
            nc.vector.tensor_scalar(part_mask[:, 0:1], ident[0:3, 0:1], 1.0, None, ALU.subtract)
            nc.vector.tensor_scalar(part_mask[:, 1:2], ident[0:3, 2:3], -1.0, None, ALU.mult).then_inc(parts, 1)
            nc.vector.tensor_tensor(beta1_b2[:, :], cols[:, BETA1:BETA1 + 1], cols[:, B2:B2 + 1], ALU.add)
            dve.wait_ge(cols_mm, 1)
            nc.vector.tensor_scalar(modT[:, CA, :], banks[1][:, 0:S], 1.0, None, ALU.add)
            nc.vector.tensor_scalar(modT[:, SABO, :], banks[1][:, S:2 * S], cols[:, BO:BO + 1], None, ALU.add)
            nc.vector.tensor_copy(modT[:, SA, :], banks[1][:, S:2 * S]).then_inc(cols_ok, 1)
            normalise("n1", n1[0], x_chunk(0, 0), 1, n1_ok)
            dve.wait_ge(bias_mm, 1)
            nc.vector.tensor_tensor(bq_col[:, :], cols[:, BQ:BQ + 1], banks[6][:, 0:1], ALU.subtract).then_inc(bq_ok, 1)
            dve.wait_ge(bias_loaded, 16)
            nc.vector.scalar_tensor_tensor(bias_k[:, :], bias3[:, :], 1.0, banks[6][0:3, D:2 * D], ALU.add,
                                           ALU.subtract).then_inc(parts, 1)
            source = bias_k
            for i in range(2):
                dve.wait_ge(parts, 2 + 2 * i)
                nc.vector.tensor_copy(high[i][:, :], source[:, :]).then_inc(parts, 1)
                dve.wait_ge(parts, 3 + 2 * i)
                dest = bias_parts if i else rest
                nc.vector.scalar_tensor_tensor(dest[:, :], high[i][:, :], part_mask[:, i:i + 1], source[:, :], ALU.mult,
                                               ALU.add).then_inc(parts, 1)
                source = rest
            dve.wait_ge(bv_loaded, 16)
            dve.wait_ge(bv_mm, 1)
            nc.vector.tensor_tensor(bv_rows[:, :], banks[3][0:S, 0:D], bv_in_rows[:, :], ALU.add).then_inc(bv_ok, 1)

            def second_columns():
                dve.wait_ge(cols_mm, 2)
                nc.vector.tensor_scalar(modT[:, CB, :], banks[2][:, 0:S], 1.0, None, ALU.add)
                nc.vector.tensor_copy(modT[:, SB, :], banks[2][:, S:2 * S]).then_inc(cols_ok, 1)

            def shift_columns():
                dve.wait_ge(cols_ok, 2)
                for i in range(2):
                    mu = cols[:, MU + i:MU + i + 1]
                    nc.vector.tensor_scalar(modT[:, FIRST + i, :], modT[:, SB, :], mu, None, ALU.mult)
                    last = nc.vector.tensor_scalar(modT[:, MOVE + i, :], modT[:, CB, :], mu, None, ALU.mult)
                last.then_inc(shift_cols, 1)
                dve.wait_ge(shift_cols, 1)
                nc.vector.tensor_tensor(modT[:, KEEP:KEEP + 2, :], modT[:, CB:CB + 1, :].broadcast_to([128, 2, S]),
                                        modT[:, MOVE:MOVE + 2, :], ALU.subtract).then_inc(shift_cols, 1)

            def take_n3(j, off):
                sp_ = 2 * j + off - 3
                need(dve, h2T_mm, sp_)
                normalise("n3", n3, lambda c: x2[(off - 3) % 2][:, c, :], sp_ + 1, n3_ok)

            def step_end(j, off):
                t = 2 * j + off
                sd, sc = t - 2, t - 4
                z = chunked(banks[6])
                if live(j, off - 2):
                    need(dve, z_mm, sd + 1)
                    norm_stats("z", lambda c: z[:, c, :])
                z_first = isinstance(j, int) and t == S + 1
                if z_first:
                    norm_mv("z", sd + 1)
                    take_n3(j, off)
                if live(j, off - 4):
                    need(dve, tanh_ok, sc + 1)
                    need(dve, v_mm, sc + 1)
                    if isinstance(j, int) and sc == S - 1:
                        dve.wait_ge(out_ok, S - 1)
                        dve.wait_ge(stored, 16 * (S - 1))
                        for c, signal in enumerate((prod_ok, last_ok)):
                            nc.vector.scalar_tensor_tensor(prod[:, c, :], tanh_r[:, c, :], 1.0, banks[5][:, c * D:(c + 1) * D],
                                                           ALU.add, ALU.mult).then_inc(signal, 1)
                        dve.wait_ge(last_ok, 1)
                        nc.vector.tensor_tensor(out_sb[:, 1, :], x2[(S - 1) % 2][:, 1, :], prod[:, 1, :],
                                                ALU.add).then_inc(last_ok, 1)
                    else:
                        nc.vector.scalar_tensor_tensor(prod[:, :, :], tanh_r[:, :, :], 1.0, chunked(banks[5]), ALU.add,
                                                       ALU.mult).then_inc(prod_ok, 1)
                if live(j, off - 2) and not z_first:
                    norm_mv("z", sd + 1)

            def step(j, off):
                t = 2 * j + off
                sa, sb_, sd, sp_, sc = t, t - 1, t - 2, t - 3, t - 4
                u = banks[1][:, 0:NC * (D + H)].rearrange("p (c e) -> p c e", c=NC)
                y = chunked(banks[1])
                z = chunked(banks[6])
                x2_p = x2[(off - 3) % 2]
                step_end(j, off - 1)
                def q_elu():
                    need(dve, expq_ok, sa + 1)
                    nc.vector.scalar_tensor_tensor(qT[:, :], exp_q[:, :], 1.0, relu_q[:, :], ALU.min,
                                                   ALU.add).then_inc(q_ok, 1)

                def mix(i):
                    need(dve, keep_ok, sc + 1)
                    nc.vector.scalar_tensor_tensor(mixT[:, i, :], banks[2][:, 0:L], modT[:, MOVE + i, bass.ds(sc, 1)],
                                                   keepT[:, i, :], ALU.mult, ALU.add).then_inc((mix_ok, mixk_ok)[i], 1)

                def attention():
                    need(dve, rden_ok, sb_ + 1)
                    for c in range(NC):
                        last = nc.vector.tensor_tensor(att[:, c, :].rearrange("p (h d) -> p h d", h=H),
                                                       u[:, c, 0:D].rearrange("p (h d) -> p h d", h=H),
                                                       rden[:, c, :].unsqueeze(2).broadcast_to([128, H, DH]), ALU.mult)
                    last.then_inc(att_ok, 1)

                y_first = isinstance(j, int) and t == S

                def y_stats():
                    need(dve, y_mm, sb_ + 1)
                    norm_stats("ny", lambda c: y[:, c, :])

                def next_n1():
                    need(dve, aks_mm, sa)
                    normalise("n1", n1[(off + 1) % 2], x_chunk(j, off + 1), sa + 2, n1_ok)

                if live(j, off + 1):
                    if isinstance(j, int) and t in (0, 3):
                        dve.wait_ge(x_in[1 if t == 0 else 2], 16)
                    norm_stats("n1", x_chunk(j, off + 1))
                    need(dve, stats_ok["n1"], sa + 2)
                if live(j, off - 1):
                    need(dve, u_mm, sb_ + 1)
                    nc.vector.tensor_scalar(den[:, :, :], u[:, :, D:D + H], EPS_ATTN, None, ALU.add).then_inc(den_ok, 1)
                if live(j, off + 1):
                    norm_mv("n1")
                if live(j, off - 1):
                    need(dve, den_ok, sb_ + 1)
                    nc.vector.reciprocal(rden[:, :, :], den[:, :, :]).then_inc(rden_ok, 1)
                if isinstance(j, int) and t == S:
                    attention()
                if draining(j, off) and t != S + 2:
                    mix(1)
                    mix(0)
                if live(j, off - 3):
                    need(dve, rstd_ok["z"], sp_ + 1)
                    for c in range(NC):
                        last = nc.vector.scalar_tensor_tensor(z1[:, c, :], z[:, c, :], mv["z"][:, c, 0:1],
                                                              gm_rows[(off - 3) % 2][:, G_ROW, :], ALU.subtract, ALU.mult)
                    last.then_inc(z1_ok, 1)
                if live(j, off - 1) and not draining(j, off):
                    attention()
                if live(j, off):
                    need(dve, expk_ok, sa + 1)
                    nc.vector.scalar_tensor_tensor(k_sb[:, :, :], exp_k[:, :, :], 1.0, chunked(banks[4]), ALU.min,
                                                   ALU.max).then_inc(k_ok, 1)
                if live(j, off - 3):
                    need(dve, xb_ok, sp_ + 1)
                    need(dve, out_ok, sp_ - 1)
                    need(dve, z1_ok, sp_ + 1)
                    for c in range(NC):
                        last = nc.vector.scalar_tensor_tensor(x2_p[:, c, :], z1[:, c, :], rstd["z"][:, c:c + 1],
                                                              xb[:, c, :], ALU.mult, ALU.add)
                    last.then_inc(x2_ok, 1)
                    if y_first:
                        y_stats()
                    need(dve, x2_ok, sp_ + 1)
                    norm_stats("n3", lambda c: x2_p[:, c, :])
                    if y_first:
                        norm_mv("ny", sb_ + 1)
                if isinstance(j, int) and t == 1:
                    second_columns()
                    gate_columns()
                if live(j, off - 4) and not draining(j, off):
                    mix(1)
                    mix(0)
                if isinstance(j, int) and t == S + 2:
                    mix(1)
                if live(j, off - 3):
                    norm_mv("n3", sp_ + 1)
                if isinstance(j, int) and t == S + 2:
                    mix(0)
                if isinstance(j, int) and t < 3:
                    q_elu()
                if live(j, off + 1) and not (isinstance(j, int) and t == 1):
                    next_n1()
                if live(j, off - 1) and not y_first:
                    y_stats()
                if live(j, off) and not (isinstance(j, int) and t < 3):
                    q_elu()
                if live(j, off - 1) and not y_first:
                    norm_mv("ny", sb_ + 1)
                if isinstance(j, int) and t == 1:
                    next_n1()
                if y_first:
                    normalise("ny", ny, lambda c: y[:, c, :], sb_ + 1, ny_ok)
                if live(j, off - 3) and not (isinstance(j, int) and t == S + 1):
                    take_n3(j, off)
                if live(j, off):
                    need(dve, a_ok, sa + 1)
                    need(dve, bv_in[off % 2], 16 * (j + off // 2 + 1), 16 * S)
                    need(dve, kv_mm, sa + 1)
                    nc.vector.scalar_tensor_tensor(kv_raw[:, :], bv_row[off % 2][:, :], ksum, banks[3][:, 0:D],
                                                   ALU.mult, ALU.add).then_inc(kvr_ok, 1)
                if live(j, off - 1) and not y_first:
                    normalise("ny", ny, lambda c: y[:, c, :], sb_ + 1, ny_ok)
                if isinstance(j, int) and t == 1:
                    dve.wait_ge(b1_mm, 1)
                    nc.vector.tensor_tensor(b1_cols[:, :], cols[:, B1:B1 + FF], banks[6][:, 0:FF], ALU.subtract).then_inc(b1_ok, 1)
                    shift_columns()

            steps(dve, step)
            step_end(0, S + STEPS_DEEP - 1)

        @block.tensor
        def _(pe):
            pe.wait_ge(warm_ok, 1)

            def keep_warm(count):
                for _ in range(count):
                    nc.tensor.matmul(banks[7][:, 0:128], warm[:, :], warm[:, :], start=True, stop=True)

            keep_warm(WARM)

            def modulation_columns(bank, chunks):
                for i, chunk in enumerate(chunks):
                    last = nc.tensor.matmul(bank[:, i * S:(i + 1) * S], wmod[:, chunk * D:(chunk + 1) * D], siluT[:, :],
                                            start=True, stop=True)
                last.then_inc(cols_mm, 1)

            pe.wait_ge(silu_ok, 2)
            pe.wait_ge(wmod_loaded[0], 16)
            modulation_columns(banks[1], (1, 0))
            keep_warm(1)
            pe.wait_ge(kq_loaded, 16)
            nc.tensor.matmul(banks[6][:, 0:1], wq, cols[:, BO:BO + 1], start=True, stop=True)
            nc.tensor.matmul(banks[6][0:3, D:2 * D], cols[:, BO:BO + 3], wk, start=True, stop=True).then_inc(bias_mm, 1)

            keep_warm(1)

            def second_modulation():
                pe.wait_ge(wmod_loaded[1], 16)
                modulation_columns(banks[2], (4, 3, 2, 5))

            def turn_gates():
                pe.wait_ge(gate_ok, 4)
                for i in range(3):
                    last = nc.tensor.transpose(banks[2][0:S, (1 + i) * D:(2 + i) * D], gate_cols[:, i, :], ident[:, :])
                last.then_inc(gates_turned, 1)

            def hidden_bias():
                pe.wait_ge(w12_loaded, 16)
                for f in range(FF):
                    last = nc.tensor.matmul(banks[6][:, f:f + 1], w1[:, f * 128:(f + 1) * 128], cols[:, B2:B2 + 1],
                                            start=True, stop=True)
                last.then_inc(b1_mm, 1)

            def bv_product():
                pe.wait_ge(cols_ok, 1)
                pe.wait_ge(wvo_loaded, 16)
                nc.tensor.matmul(banks[3][0:S, 0:D], modT[:, SA, :], wv, start=True, stop=True).then_inc(bv_mm, 1)

            def transpose_in(bank, tile, signal):
                for c in range(NC):
                    last = nc.tensor.transpose(bank[:, c * 128:(c + 1) * 128], tile[:, c, :], ident[:, :])
                last.then_inc(signal, 1)

            def residual_into(bank, tileT, c):
                return nc.tensor.matmul(bank[:, c * D:(c + 1) * D], tileT[:, c * 128:(c + 1) * 128], ident[:, :],
                                        start=(c == 0), stop=False, is_transpose=True)

            def feed_forward_out(f0, f1):
                for f in range(f0, f1):
                    for c in range(NC):
                        last = nc.tensor.matmul(banks[6][:, c * D:(c + 1) * D], hid[:, f, c * 128:(c + 1) * 128], w2[:, f, :],
                                                start=False, stop=(f == FF - 1 and c == NC - 1))
                return last

            def n3_transposes(j, off):
                sc = 2 * j + off - 4
                need(pe, n3_ok, sc + 1)
                need(pe, mix_ok, sc)
                transpose_in(banks[2], n3, h2T_mm)

            def mix_products(j, off):
                sc = 2 * j + off - 4
                if live(j, off - 4):
                    if isinstance(j, int) and sc == 0:
                        pe.wait_ge(mix_loaded, 16)
                    need(pe, attT_ok, sc + 4)
                    need(pe, mixk_ok, sc + 1)
                    nc.tensor.matmul(banks[0][:, 0:L], wkT, mixT[:, 1, :], start=True, stop=True).then_inc(kk_mm, 1)
                    need(pe, mix_ok, sc + 1)
                    need(pe, k_ok, sc + 5)
                    for c in range(NC):
                        last = nc.tensor.matmul(banks[4][:, c * D:(c + 1) * D], mixT[:, 0, c * 128:(c + 1) * 128], wrT,
                                                start=True, stop=True)
                    last.then_inc(r_mm, 1)

            def step(j, off):
                t = 2 * j + off
                sa, sb_, sd, sc = t, t - 1, t - 2, t - 4

                def hidden_product(f):
                    bank = hidden_bank(j, off) if f >= 2 else banks[7]
                    return nc.tensor.matmul(bank[:, f % 2 * L:(f % 2 + 1) * L], w1[:, f * 128:(f + 1) * 128], x1T[:, :],
                                            start=True, stop=True)

                if live(j, off):
                    need(pe, n1_ok, sa + 1)
                    need(pe, attT_ok, sa - 1)
                    need(pe, reluk_ok, sa - 4)
                    if isinstance(j, int) and t == 0:
                        pe.wait_ge(const_pool, 3)
                    transpose_in(banks[0], n1[off % 2], hT_mm)
                    if isinstance(j, int) and t == 1:
                        keep_warm(1)
                        second_modulation()
                        keep_warm(1)
                    if isinstance(j, int) and t == 0:
                        bv_product()
                        keep_warm(1)
                        pe.wait_ge(parts, 6)
                if live(j, off - 2):
                    need(pe, ny_ok, sd + 1)
                    need(pe, hida_ok, sd)
                    transpose_in(banks[7], ny, x1T_mm)
                if live(j, off - 4):
                    if isinstance(j, int) and sc == 0:
                        pe.wait_ge(rows_ok, 1)
                    if isinstance(j, int) and t == S + 2:
                        keep_warm(2)
                    if not (isinstance(j, int) and t == S + 3):
                        n3_transposes(j, off)
                    if isinstance(j, int) and t >= S + 2:
                        keep_warm(5)
                if live(j, off - 1):
                    need(pe, s16_ok, sb_ + 1)
                    need(pe, kv_ok, sb_ + 1)
                    need(pe, q_ok, sb_ + 1)
                    need(pe, ny_ok, sb_)
                    for c in range(NC):
                        last = nc.tensor.matmul(banks[1][:, c * (D + H):(c + 1) * (D + H)], qT[:, c * 128:(c + 1) * 128],
                                                kvs[:, :], start=True, stop=True)
                    last.then_inc(u_mm, 1)
                if live(j, off):
                    need(pe, hT_ok, sa + 1)
                    need(pe, k_ok, sa)
                    need(pe, tanh_ok, sa - 4)
                    nc.tensor.matmul(chunked(banks[4]), ones3[:, :], bias_parts[:, :].unsqueeze(1).broadcast_to([3, NC, D]),
                                     start=True, stop=False)
                    for c in range(NC):
                        last = nc.tensor.matmul(banks[4][:, c * D:(c + 1) * D], hT[off % 2][:, c * 128:(c + 1) * 128],
                                                wk, start=False, stop=(c == NC - 1))
                    last.then_inc(k_mm, 1)
                    need(pe, q_ok, sa)
                    need(pe, prod_ok, sa - 4)
                    nc.tensor.matmul(banks[5][:, 0:L], wq, hT[off % 2][:, :], start=True, stop=True).then_inc(q_mm, 1)
                    if isinstance(j, int) and t == 0:
                        keep_warm(1)
                if live(j, off - 2):
                    need(pe, x1T_ok, sd + 1)
                    hidden_product(0)
                    hidden_product(1).then_inc(w1a_mm, 1)
                    if isinstance(j, int) and sd == 0:
                        pe.wait_ge(b1_ok, 1)
                    if draining(j, off):
                        need(pe, kvr_ok, S)
                        need(pe, hidb_ok, sd)
                    else:
                        need(pe, z1_ok, sd)
                    hidden_product(2)
                if live(j, off - 1):
                    need(pe, att_ok, sb_ + 1)
                    need(pe, hT_ok, sb_ + 2)
                    need(pe, reluk_ok, sb_ - 3)
                    transpose_in(banks[0], att, attT_mm)
                if live(j, off - 2):
                    hidden_product(3).then_inc(w1b_mm, 1)
                if live(j, off):
                    need(pe, k_ok, sa + 1)
                    need(pe, kvr_ok, sa)
                    for c in range(NC):
                        nc.tensor.matmul(banks[3][:, 0:D], n1[off % 2][:, c, :], k_sb[:, c, :], start=(c == 0),
                                         stop=(c == NC - 1))
                if live(j, off - 1):
                    need(pe, attT_ok, sb_ + 1)
                    for c in range(NC):
                        residual_into(banks[1], hT[(off - 1) % 2], c)
                        last = nc.tensor.matmul(banks[1][:, c * D:(c + 1) * D], attT[:, c * 128:(c + 1) * 128], wo,
                                                start=False, stop=(c == NC - 1))
                    last.then_inc(y_mm, 1)
                if live(j, off):
                    need(pe, pair_ok, sa + 1)
                    nc.tensor.matmul(banks[3][:, D:D + 1], k_pair[:, :], ones[:, :], start=True, stop=True).then_inc(aks_mm, 1)
                    if isinstance(j, int) and t == 0:
                        keep_warm(2)
                if isinstance(j, int) and t == 1:
                    hidden_bias()
                    turn_gates()
                mix_products(j, off)
                z_first = isinstance(j, int) and t == S + 1
                if live(j, off - 2):
                    if draining(j, off):
                        need(pe, z1_ok, sd)
                        need(pe, hida_ok, sd + 1)
                    else:
                        need(pe, hidb_ok, sd + 1)
                    for c in range(NC):
                        residual_into(banks[6], x1T, c)
                if live(j, off):
                    need(pe, a_ok, sa + 1)
                    need(pe, wvm_ok, sa + 1)
                    nc.tensor.matmul(banks[3][:, 0:D], a_sb[:, 0:D], wv_mod[:, :], start=True, stop=True).then_inc(kv_mm, 1)
                if live(j, off - 2):
                    feed_forward_out(0, 2)
                if z_first:
                    need(pe, hidb_ok, sd + 1)
                    feed_forward_out(2, FF).then_inc(z_mm, 1)
                if isinstance(j, int) and t == S + 2:
                    n3_transposes(j, off + 1)
                if live(j, off - 4):
                    need(pe, ksq_ok, sc + 1)
                    need(pe, wvg_ok, sc + 1)
                    need(pe, q_ok, sc + 5)
                    for c in range(NC):
                        last = nc.tensor.matmul(banks[5][:, c * D:(c + 1) * D], ksqT[:, c * 128:(c + 1) * 128], wv_gate[:, :],
                                                start=True, stop=True)
                    last.then_inc(v_mm, 1)
                if live(j, off - 2) and not z_first:
                    if draining(j, off):
                        need(pe, hidb_ok, sd + 1)
                    feed_forward_out(2, FF).then_inc(z_mm, 1)

            steps(pe, step)


def kernel(**inputs):
    import concourse.bacc as bacc
    from concourse.bass_utils import run_bass_kernel_spmd

    nc = bacc.Bacc("TRN2", target_bir_lowering=False, num_devices=1)
    attn = {n: inputs[f"L0_attn_{n}"] for n in ("x", "Wq", "bq", "Wk", "bk", "Wv", "bv", "Wo", "bo", "W1", "b1", "W2", "b2",
                                               "g1", "beta1", "g2", "beta2")}
    ffn = {n: inputs[f"L0_ffn_{n}"] for n in ("W_r", "W_k", "W_v", "mu_r", "mu_k")}
    laid_out = {
        "x": attn["x"],
        "wmod": inputs["L0_wmod"],
        "cols": np.concatenate([np.asarray(inputs["L0_c"]).T]
                               + [np.reshape(v, (-1, 128)).T for v in (
                                   attn["g1"], attn["beta1"], ffn["mu_r"], ffn["mu_k"], attn["b1"], attn["bq"],
                                   attn["b2"], attn["g2"], attn["beta2"], attn["bo"], attn["bo"], attn["bo"])], axis=1),
        "kqvo": np.stack([attn[n] for n in ("Wk", "Wq", "Wv", "Wo")], axis=1),
        "w12": np.stack([attn["W1"], np.reshape(attn["W2"], (FF, 128, D)).transpose(1, 0, 2).reshape(128, FF * D)], axis=1),
        "mix_w": np.stack([np.asarray(ffn[n]).T for n in ("W_r", "W_k", "W_v")], axis=1),
        "bk": attn["bk"],
        "bv": attn["bv"],
    }
    arrays, aps = {}, {}
    for name, arr in laid_out.items():
        arr = np.ascontiguousarray(arr)
        arrays[f"in_{name}"] = arr
        aps[name] = nc.dram_tensor(f"in_{name}", arr.shape, mybir.dt.from_np(arr.dtype), kind="ExternalInput").ap()
    out = nc.dram_tensor("out", (S, L, D), F32, kind="ExternalOutput").ap()
    scratch = {"bv": nc.dram_tensor("bv_rows_dram", (S, D), F32, kind="Internal").ap(),
               "rows": nc.dram_tensor("mod_rows_dram", (S, 3, D), F32, kind="Internal").ap()}
    build(nc, aps, out, scratch)
    r = run_bass_kernel_spmd(nc, [arrays], core_ids=[0])
    return r.results[0]["out"]
```
